# Optimizing a Trainium2 kernel written in Bass

```python
import numpy as np
import jax
import jax.numpy as jnp

def _softmax(x, axis=-1):
    return jax.nn.softmax(x, axis=axis)

def _gelu(x):
    return jax.nn.gelu(x, approximate=True)

def _silu(x):
    return jax.nn.silu(x)

def _sigmoid(x):
    return jax.nn.sigmoid(x)

def _layernorm(x, axis=-1, eps=1e-05):
    m = jnp.mean(x, axis=axis, keepdims=True)
    v = jnp.var(x, axis=axis, keepdims=True)
    return (x - m) / jnp.sqrt(v + eps)

def _scatter_add(tgt, idx, src, axis=0):
    return tgt.at[idx].add(src)

def _segment_sum(src, seg, n):
    return jax.ops.segment_sum(src, seg, n)
kernel_name = 'mk_recurrent_d1_jaxref_r8_3e0b0f'

def setup_inputs(seed: int=0):
    np.random.seed(seed)
    _w = jnp.asarray

    def _L0_attn_setup():
        import jax, jax.numpy as jnp
        import numpy as np
        DIM = 128
        HEADS = 16
        BATCH = 2
        SEQ = 256
        key = jax.random.key(seed)
        ks = jax.random.split(key, 7)
        s = DIM ** (-0.5)
        return {'x': jax.random.normal(ks[0], (BATCH, SEQ, DIM), dtype=jnp.float32), 'Wq': jax.random.normal(ks[1], (DIM, DIM), dtype=jnp.float32) * s, 'Wk': jax.random.normal(ks[2], (DIM, DIM), dtype=jnp.float32) * s, 'Wv': jax.random.normal(ks[3], (DIM, DIM), dtype=jnp.float32) * s, 'Wo': jax.random.normal(ks[4], (DIM, DIM), dtype=jnp.float32) * s, 'compressibility': jnp.ones((HEADS, 1, 1), dtype=jnp.float32) * 0.5, 'phase_threshold': jnp.zeros((HEADS, 1, 1), dtype=jnp.float32)}
    _L0_attn_in = _L0_attn_setup()

    def _L0_ffn_setup():
        import jax, jax.numpy as jnp
        import numpy as np
        D_MODEL = 128
        N_HEADS = 16
        D_HEAD = D_MODEL // N_HEADS
        N_EXPERTS = 8
        TOP_K = 2
        D_FF = 256
        EPS = 1e-06

        def rmsnorm(x, w):
            return x * jax.lax.rsqrt(jnp.mean(x * x, axis=-1, keepdims=True) + EPS) * w

        def swiglu(x, w_gate, w_up, w_down):
            return jax.nn.silu(x @ w_gate) * (x @ w_up) @ w_down
        key = jax.random.key(seed)
        ks = jax.random.split(key, 16)
        s = 0.02
        B, S = (2, 256)
        return {'X': jax.random.normal(ks[0], (B, S, D_MODEL), dtype=jnp.float32), 'norm1_w': jnp.ones((D_MODEL,), jnp.float32), 'norm2_w': jnp.ones((D_MODEL,), jnp.float32), 'wq': jax.random.normal(ks[1], (D_MODEL, D_MODEL), jnp.float32) * s, 'wk': jax.random.normal(ks[2], (D_MODEL, D_MODEL), jnp.float32) * s, 'wv': jax.random.normal(ks[3], (D_MODEL, D_MODEL), jnp.float32) * s, 'wo': jax.random.normal(ks[4], (D_MODEL, D_MODEL), jnp.float32) * s, 'router_w': jax.random.normal(ks[5], (D_MODEL, N_EXPERTS), jnp.float32) * s, 'sh_gate': jax.random.normal(ks[6], (D_MODEL, D_FF), jnp.float32) * s, 'sh_up': jax.random.normal(ks[7], (D_MODEL, D_FF), jnp.float32) * s, 'sh_down': jax.random.normal(ks[8], (D_FF, D_MODEL), jnp.float32) * s, 'e_gate': jax.random.normal(ks[9], (N_EXPERTS, D_MODEL, D_FF), jnp.float32) * s, 'e_up': jax.random.normal(ks[10], (N_EXPERTS, D_MODEL, D_FF), jnp.float32) * s, 'e_down': jax.random.normal(ks[11], (N_EXPERTS, D_FF, D_MODEL), jnp.float32) * s}
    _L0_ffn_in = _L0_ffn_setup()
    _d = {'L0_attn_x': _L0_attn_in['x'], 'L0_attn_Wq': _L0_attn_in['Wq'], 'L0_attn_Wk': _L0_attn_in['Wk'], 'L0_attn_Wv': _L0_attn_in['Wv'], 'L0_attn_Wo': _L0_attn_in['Wo'], 'L0_attn_compressibility': _L0_attn_in['compressibility'], 'L0_attn_phase_threshold': _L0_attn_in['phase_threshold'], 'L0_ffn_norm1_w': _L0_ffn_in['norm1_w'], 'L0_ffn_norm2_w': _L0_ffn_in['norm2_w'], 'L0_ffn_wq': _L0_ffn_in['wq'], 'L0_ffn_wk': _L0_ffn_in['wk'], 'L0_ffn_wv': _L0_ffn_in['wv'], 'L0_ffn_wo': _L0_ffn_in['wo'], 'L0_ffn_router_w': _L0_ffn_in['router_w'], 'L0_ffn_sh_gate': _L0_ffn_in['sh_gate'], 'L0_ffn_sh_up': _L0_ffn_in['sh_up'], 'L0_ffn_sh_down': _L0_ffn_in['sh_down'], 'L0_ffn_e_gate': _L0_ffn_in['e_gate'], 'L0_ffn_e_up': _L0_ffn_in['e_up'], 'L0_ffn_e_down': _L0_ffn_in['e_down']}
    _x0 = _d['L0_attn_x']
    _d['L0_attn_x'] = jax.random.normal(jax.random.fold_in(jax.random.key(seed), 1), (8, 512, 128), dtype=_x0.dtype)
    del _x0
    return _d

def reference(L0_attn_x, L0_attn_Wq, L0_attn_Wk, L0_attn_Wv, L0_attn_Wo, L0_attn_compressibility, L0_attn_phase_threshold, L0_ffn_norm1_w, L0_ffn_norm2_w, L0_ffn_wq, L0_ffn_wk, L0_ffn_wv, L0_ffn_wo, L0_ffn_router_w, L0_ffn_sh_gate, L0_ffn_sh_up, L0_ffn_sh_down, L0_ffn_e_gate, L0_ffn_e_up, L0_ffn_e_down):

    def _L0_attn_ref(x, Wq, Wk, Wv, Wo, compressibility, phase_threshold):
        import jax, jax.numpy as jnp
        import numpy as np
        DIM = 128
        HEADS = 16
        BATCH = 2
        SEQ = 256
        b, l, d = x.shape
        h = compressibility.shape[0]
        hd = d // h
        scale = hd ** (-0.5)

        def proj(W):
            return (x @ W.T).reshape(b, l, h, hd).transpose(0, 2, 1, 3)
        q, k, v = (proj(Wq), proj(Wk), proj(Wv))
        pressure = jnp.einsum('bhid,bhjd->bhij', q, k) * scale
        causal = jnp.triu(jnp.ones((l, l), dtype=bool), k=1)
        pressure = jnp.where(causal, jnp.float32(-10000.0), pressure)
        tau = jax.nn.softplus(compressibility) + 1e-06
        energy = (pressure - phase_threshold) / tau
        attn = 1.0 - jnp.tanh(energy) ** 2
        attn = attn / (jnp.sum(attn, axis=-1, keepdims=True) + 1e-06)
        out = jnp.einsum('bhij,bhjd->bhid', attn, v)
        out = out.transpose(0, 2, 1, 3).reshape(b, l, d)
        return out @ Wo.T

    def _L0_ffn_ref(X, norm1_w, norm2_w, wq, wk, wv, wo, router_w, sh_gate, sh_up, sh_down, e_gate, e_up, e_down):
        import jax, jax.numpy as jnp
        import numpy as np
        D_MODEL = 128
        N_HEADS = 16
        D_HEAD = D_MODEL // N_HEADS
        N_EXPERTS = 8
        TOP_K = 2
        D_FF = 256
        EPS = 1e-06

        def rmsnorm(x, w):
            return x * jax.lax.rsqrt(jnp.mean(x * x, axis=-1, keepdims=True) + EPS) * w

        def swiglu(x, w_gate, w_up, w_down):
            return jax.nn.silu(x @ w_gate) * (x @ w_up) @ w_down
        B, S, d = X.shape
        scale = 1.0 / jnp.sqrt(jnp.asarray(D_HEAD, X.dtype))
        h = rmsnorm(X, norm1_w)
        q = (h @ wq).reshape(B, S, N_HEADS, D_HEAD)
        k = (h @ wk).reshape(B, S, N_HEADS, D_HEAD)
        v = (h @ wv).reshape(B, S, N_HEADS, D_HEAD)
        scores = jnp.einsum('bshd,bthd->bhst', q, k) * scale
        attn = jax.nn.softmax(scores, axis=-1)
        ctx = jnp.einsum('bhst,bthd->bshd', attn, v).reshape(B, S, d)
        X = X + ctx @ wo
        h2 = rmsnorm(X, norm2_w).reshape(B * S, d)
        logits = h2 @ router_w
        probs = jax.nn.softmax(logits, axis=-1)
        topw, topi = jax.lax.top_k(probs, TOP_K)
        topw = jax.nn.softmax(topw, axis=-1)
        combine = jnp.sum(jax.nn.one_hot(topi, N_EXPERTS, dtype=h2.dtype) * topw[..., None], axis=1)
        shared = swiglu(h2, sh_gate, sh_up, sh_down)
        gate = jnp.einsum('td,edf->etf', h2, e_gate)
        up = jnp.einsum('td,edf->etf', h2, e_up)
        eout = jnp.einsum('etf,efd->etd', jax.nn.silu(gate) * up, e_down)
        spec = jnp.einsum('etd,te->td', eout, combine)
        moe_out = (shared + spec).reshape(B, S, d)
        return X + moe_out
    x = L0_attn_x
    xn = _layernorm(x, axis=-1)
    s = _L0_attn_ref(xn, L0_attn_Wq, L0_attn_Wk, L0_attn_Wv, L0_attn_Wo, L0_attn_compressibility, L0_attn_phase_threshold)
    g = _silu(_L0_ffn_ref(xn, L0_ffn_norm1_w, L0_ffn_norm2_w, L0_ffn_wq, L0_ffn_wk, L0_ffn_wv, L0_ffn_wo, L0_ffn_router_w, L0_ffn_sh_gate, L0_ffn_sh_up, L0_ffn_sh_down, L0_ffn_e_gate, L0_ffn_e_up, L0_ffn_e_down))
    x = x + s * g
    return x

_drawn_inputs = setup_inputs


def setup_inputs(seed=0):
    import zlib

    import numpy as np

    out = dict(_drawn_inputs(seed))
    spreads = {'L0_attn_compressibility': (0.5, 0.6),
     'L0_attn_phase_threshold': (0.0, 0.8),
     'L0_ffn_norm1_w': (1.0, 0.6),
     'L0_ffn_norm2_w': (1.0, 0.6)}
    factors = {'L0_ffn_wq': 8.0,
     'L0_ffn_wk': 8.0,
     'L0_ffn_wv': 8.0,
     'L0_ffn_wo': 8.0,
     'L0_ffn_router_w': 8.0,
     'L0_ffn_sh_gate': 8.0,
     'L0_ffn_sh_up': 8.0,
     'L0_ffn_sh_down': 8.0,
     'L0_ffn_e_gate': 8.0,
     'L0_ffn_e_up': 8.0,
     'L0_ffn_e_down': 8.0}
    for name, (base, spread) in spreads.items():
        noise = np.random.default_rng([zlib.crc32(name.encode()), seed]).standard_normal(out[name].shape)
        drawn = base * np.exp(spread * noise) if base else spread * noise
        out[name] = jnp.asarray(drawn.astype(out[name].dtype))
    for name, factor in factors.items():
        out[name] = (out[name] * factor).astype(out[name].dtype)
    return out
```

```python
import concourse.bass as bass
from concourse import mybir
from contextlib import ExitStack

B, L, D = 8, 512, 128
H, HD = 16, 8
E, F = 8, 256
NE = E + 1
NT = L // 128
NG = H // 4
VW = 12
NFH = F // 128
PAIRS = [(0, 0), (0, 1), (0, 2), (1, 0), (1, 1), (2, 0)]
ROW_ADD = 64
UNITS = 4 * NG
HX = 12
MASKED = -10000.0

MAX_Y = [(h, t) for h in range(HX, H) for t in range(NT)]
MAX_X = [(h, t) for h in range(HX) for t in range(NT)]
Y_AT = {0: MAX_Y[0:6], 1: MAX_Y[6:12], 2: MAX_Y[12:16]}
X_AT = {e: MAX_X[7 * (e - 1):7 * e] for e in range(1, 8)}


def work_slots(own, following):
    order = []
    if own:
        for u in range(3):
            order += [("max", h, t) for h, t in Y_AT[u]]
        order += ["maxT_Y"] + [("oT2", t) for t in range(NT)] + ["ctxT2", "proj2", "h2T"]
    if following:
        order += ["xnT", "hT"]
    if own:
        order += ["logits"]
    if following:
        order += ["Q2", "K2", "V2", "Q1", "K1"]
    if own:
        order += ["suffix", "combT", ("oT1", 0), ("oT1", 1)]
    if following:
        order += [("max", h, t) for h, t in X_AT[1]]
    if own:
        order += [("oT1", 2), ("oT1", 3)]
    if following:
        order += [("max", h, t) for h, t in X_AT[2]]
    if own:
        order += ["ctxT1"]
    if following:
        order += ["V1"] + [("max", h, t) for h, t in X_AT[3]]
    if own:
        order += ["proj1"]
    if following:
        for e in range(4, 8):
            order += [("max", h, t) for h, t in X_AT[e]]
        order += ["maxT_X"]
    if own:
        order += ["outT"]
    return order


class Uses:

    def __init__(self, own, following, before=(0, 0)):
        self.order = work_slots(own, following)
        self.at = {name: n for n, name in enumerate(self.order)}
        self.total = [(len(self.order) + 1) // 2, len(self.order) // 2]
        self.before = before

    def __call__(self, name):
        n = self.at[name]
        return n % 2, self.before[n % 2] + n // 2

    def row(self, it):
        later = Uses.__new__(Uses)
        later.order, later.at, later.total = self.order, self.at, self.total
        later.before = tuple(b + it * t for b, t in zip(self.before, self.total))
        return later


FIRST = Uses(False, True)
LOOP = Uses(True, True, FIRST.total)
LAST = Uses(True, False, LOOP.row(B - 1).before)

S_USES = (2 * NG * 4 + NG * 6 + 2 * NE) // 2
O_USES = (2 * NG // 2 + 1, 2 * NG // 2 + E)
PIECES = 6
DOWNS = NE + 1
DVE_FIRST, DVE_ROW = 31, 33
SPLIT_STEPS = 12


def program(nc, x, par, n1w, n2w, w1, w2, router, w_gu, w_dn, out):
    dt, ALU, ACT, AX = mybir.dt, mybir.AluOpType, mybir.ActivationFunctionType, mybir.AxisListType
    fp32, fp32r, bf16 = dt.float32, dt.float32r, dt.bfloat16

    ctx_ = ExitStack()
    with ctx_:
        def sb(name, shape, t=fp32):
            return ctx_.enter_context(nc.sbuf_tensor(name, shape, t))

        def sem(name):
            return ctx_.enter_context(nc.semaphore(name))

        xin = sb("xin", [128, NT, D])
        xres = sb("xres", [128, NT, D])
        xn = sb("xn", [128, NT, D])
        ht = sb("ht", [128, NT, D])
        x1 = sb("x1", [128, NT, D])
        h2t = sb("h2t", [128, NT, D])
        ctxs = ht
        ctxT = sb("ctxT", [128, L])
        xnT = sb("xnT", [128, L])
        hT = sb("hT", [128, L])
        h2T = sb("h2T", [128, L])
        h2hi = sb("h2hi", [128, L], fp32r)
        h2lo = sb("h2lo", [128, L], fp32r)
        sT = sb("sT", [128, L])
        gT = h2T
        corr = h2T[:, :].rearrange("p (t d) -> p t d", t=NT)
        split = [sb(f"split{i}", [128, L]) for i in range(2)]
        parts = [sb(f"parts{i}", [128, 3, L], bf16) for i in range(2)]
        stack = {n: sb("stack" + n, [128, H, L], bf16) for n in ("Q2", "K2", "Q1", "K1")}
        V2 = sb("V2", [128, NT, H, VW])
        V1 = sb("V1", [128, NT, H, VW])
        PT = [sb(f"PT{i}", [128, 4096]) for i in range(2)]
        AB = [PT[0][:, 0:1024], PT[0][:, 1024:2048]]
        CB = [PT[0][:, 2048:2560], PT[0][:, 2560:3072]]
        OS = sb("OS", [128, NG, L])
        cT = sb("cT", [128, L], fp32r)
        wgu_hi = sb("wgu_hi", [128, NE, 2 * F], fp32r)
        wgu_lo = sb("wgu_lo", [128, NE, 2 * F], fp32r)
        wdn = sb("wdn", [128, NE, NFH, D])
        w1s = sb("w1s", [128, 4, D])
        w2s = sb("w2s", [128, 4, D])
        rts = sb("rts", [128, E])
        n1s = sb("n1s", [128, 1])
        n2s = sb("n2s", [128, 1])
        ident = sb("ident", [128, 128])
        identb = sb("identb", [128, 128], bf16)
        below = sb("below", [128, 128])
        ones = sb("ones", [128, 128])
        sel = sb("sel", [128, E, 128], fp32r)
        nmax = sb("nmax", [128, H, NT])
        mhX = sb("mhX", [128, 2, HX * NT], bf16)
        mhY = sb("mhY", [128, 2, (H - HX) * NT], bf16)
        mTX = sb("mTX", [2 * HX * NT, 128], bf16)
        mTY = sb("mTY", [2 * (H - HX) * NT, 128], bf16)
        stats = sb("stats", [128, NT, 6])
        mv = sb("mv", [128, NT, 2])
        root = sb("root", [128, 3, NT])
        rinv = sb("rinv", [128, 3, NT])
        eps6 = sb("eps6", [128, 1])
        ssum = sb("ssum", [128, NT])
        rden = sb("rden", [128, NT, H])
        dsum = sb("dsum", [128, NT, H])
        dcorr = sb("dcorr", [128, NT, H])
        cneg = sb("cneg", [128, H])
        qs1 = sb("qs1", [128, 1])
        pars = sb("pars", [128, 2, H + 1])
        pt = [sb(f"pt{i}", [128, H + 1]) for i in range(8)]
        bparts = sb("bparts", [128, 3, H])
        bsplit = sb("bsplit", [128, 3, H], bf16)
        brow = sb("brow", [128, H])
        iota_i = sb("iota_i", [128, E], dt.int32)
        rest_i = sb("rest_i", [128, NT], dt.int32)
        iota_f = sb("iota_f", [128, E])
        rest_f = sb("rest_f", [128, NT])
        lmax = sb("lmax", [128, NT])
        ld = sb("ld", [128, NT, E])
        lp = sb("lp", [128, NT, E])
        lq = sb("lq", [128, NT, E])
        lsum = sb("lsum", [128, NT])
        top = sb("top", [128, NT, 8])
        topi = sb("topi", [128, NT, 8], dt.uint32)
        topf = sb("topf", [128, NT, 8])
        dtop = sb("dtop", [128, NT])
        wtop = sb("wtop", [128, 2, NT])
        comb = sb("comb", [128, NT, E])
        scratch = {n: nc.dram_tensor("scr" + n, [3, 128, L], bf16).ap() for n in stack}

        def pb(name, cols):
            return ctx_.enter_context(nc.psum_tensor(name, [128, cols], fp32))

        S = [pb("S0", 1024), pb("S1", 1024)]
        O = [pb("O0", 512), pb("O1", 512)]
        M = [pb("M0", 512), pb("M1", 512)]

        s_full, s_read = [sem("s_full0"), sem("s_full1")], [sem("s_read0"), sem("s_read1")]
        m_full, m_read = [sem("m_full0"), sem("m_full1")], [sem("m_read0"), sem("m_read1")]
        o_read = [sem("o_read0"), sem("o_read1")]
        pv_done = sem("pv_done")
        weighed = sem("weighed")
        masked = sem("masked")
        cb_full = sem("cb_full")
        routed = sem("routed")
        down_done = sem("down_done")
        xn_ready, h_ready, h2_ready, h2r_ready = (sem(n) for n in ("xn_ready", "h_ready", "h2_ready", "h2r_ready"))
        roots_ready, rooted1, rooted2, squared = (sem(n) for n in ("roots_ready", "rooted1", "rooted2", "squared"))
        exps_ready, gap_ready, top_ready, comb_ready = (sem(n) for n in ("exps_ready", "gap_ready", "top_ready", "comb_ready"))
        parts_ready, maxX_ready, maxY_ready, prod_ready = (sem(n) for n in ("parts_ready", "maxX_ready", "maxY_ready", "prod_ready"))
        stored = {n: sem("stored" + n) for n in stack}
        stacked = {n: sem("stacked" + n) for n in stack}
        rowX, rowY = sem("rowX"), sem("rowY")
        xin_in, xres_in, written = sem("xin_in"), sem("xres_in"), sem("written")
        par_in, w_in, gu_in, dn_in = sem("par_in"), sem("w_in"), sem("gu_in"), sem("dn_in")
        dve_step, pool_step = sem("dve_step"), sem("pool_step")
        passed = sem("passed")
        gated = sem("gated")
        cleared, shaped, counted, kset, setup, tau_step = (
            sem(n) for n in ("cleared", "shaped", "counted", "kset", "setup", "tau_step"))

        x_t = x.rearrange("b (t p) d -> b p t d", p=128)
        out_t = out.rearrange("b (t p) d -> b p t d", p=128)
        block = ctx_.enter_context(nc.Block())

        def full(u, name):
            k, n = u(name)
            return m_full[k], n + 1

        def read(u, name):
            k, n = u(name)
            return m_read[k], n + 2

        def free(u, name):
            k, n = u(name)
            return m_read[k], n + 1

        def wait_apart(engine, semaphore, value):
            engine.wait_ge(semaphore, value)
            engine.sem_inc(passed, 1)

        def score_use(it, n):
            return n % 2, it * S_USES + n // 2

        def acc_use(it, G):
            return G % 2, it * O_USES[G % 2] + G // 2

        @block.sync
        def _(sp):
            sp.dma_start(xin[:, :, :], x_t[0]).then_inc(xin_in, 16)
            sp.dma_start(pars[:, :, :], par).then_inc(par_in, 16)
            sp.dma_start(n1s[:, :], n1w).then_inc(w_in, 16)
            sp.dma_start(n2s[:, :], n2w).then_inc(w_in, 16)
            sp.dma_start(w2s[:, :, :], w2).then_inc(w_in, 16)
            sp.dma_start(w1s[:, :, :], w1).then_inc(w_in, 16)
            sp.dma_start(rts[:, :], router).then_inc(w_in, 16)

            def restack(name, i, bt):
                sp.wait_ge(parts_ready, bt * 4 + i + 1)
                sp.dma_start(scratch[name].rearrange("a p n -> p a n"), parts[i % 2][:, :, :]).then_inc(stored[name], 16)
                sp.wait_ge(stored[name], bt * 16 + 16)
                side = 0 if name[0] == "Q" else 1
                for c, pair in enumerate(PAIRS):
                    sp.dma_start(stack[name][HD * c:HD * c + HD, :, :],
                                 scratch[name][pair[side]].rearrange("(h d) n -> d h n", d=HD)).then_inc(stacked[name], 16)

            def maxima_rows(mT, rows, h0, h1):
                per = (h1 - h0) * NT
                for part in range(2):
                    row = stack["Q2"][ROW_ADD + part:ROW_ADD + part + 1, h0:h1, :]
                    sp.dma_start(row.rearrange("o h (t n) -> o (h t) n", n=128),
                                 mT[part * per:(part + 1) * per, :]).then_inc(rows, 16)

            def prepare(u, bt, it=None):
                for i, name in enumerate(("Q2", "K2")):
                    if it is not None:
                        for k in range(2):
                            wait_apart(sp, s_full[k], it * S_USES + 4 * NG)
                    restack(name, i, bt)
                for i, name in enumerate(("Q1", "K1")):
                    if it is not None:
                        for k in range(2):
                            wait_apart(sp, s_full[k], it * S_USES + 7 * NG)
                    restack(name, i + 2, bt)
                wait_apart(sp, *read(u, "maxT_X"))
                maxima_rows(mTX, rowX, 0, HX)

            def row(u, it, following):
                if following:
                    wait_apart(sp, h_ready, it + 1)
                    sp.dma_start(xin[:, :, :], x_t[bass.ds(it + 1, 1)].rearrange("o p t d -> (o p) t d")).then_inc(xin_in, 16)
                sp.dma_start(xres[:, :, :], x_t[bass.ds(it, 1)].rearrange("o p t d -> (o p) t d")).then_inc(xres_in, 16)
                wait_apart(sp, *read(u, "maxT_Y"))
                maxima_rows(mTY, rowY, HX, H)
                if following:
                    prepare(u, it + 1, it)
                wait_apart(sp, *read(u, "outT"))
                sp.dma_start(out_t[bass.ds(it, 1)].rearrange("o p t d -> (o p) t d"), xres[:, :, :]).then_inc(written, 16)
                wait_apart(sp, written, it * 16 + 16)

            sp.wait_ge(kset, 2)
            sp.wait_ge(setup, 1)
            prepare(FIRST, 0)
            with sp.Fori(0, B - 1) as it:
                row(LOOP.row(it), it, True)
            row(LAST, B - 1, False)

        @block.gpsimd
        def _(pool):
            g = nc.gpsimd
            g.memset(ident[:, :], 0.0).then_inc(cleared, 1)
            g.memset(below[:, :], 1.0).then_inc(cleared, 1)
            selv = PT[1][:, 0:E * 128].rearrange("p (e m) -> p e m", e=E)
            g.memset(selv, 0.0).then_inc(cleared, 1)
            g.memset(bparts[:, :, :], 1.0).then_inc(cleared, 1)
            g.memset(ones[:, :], 1.0).then_inc(shaped, 1)
            g.iota(iota_i[:, :], [[1, E]], base=0, channel_multiplier=0).then_inc(counted, 1)
            g.iota(rest_i[:, :], [[-128, NT]], base=L - 1, channel_multiplier=-1).then_inc(counted, 1)
            pool.wait_ge(cleared, 4)
            g.affine_select(out=ident[:, :], in_=ident[:, :], compare_op=ALU.not_equal, fill=1.0, base=0,
                            pattern=[[-1, 128]], channel_multiplier=1).then_inc(shaped, 1)
            g.affine_select(out=below[:, :], in_=below[:, :], compare_op=ALU.is_gt, fill=0.0, base=0,
                            pattern=[[-1, 128]], channel_multiplier=1).then_inc(shaped, 1)
            g.affine_select(out=bparts[:, :, :], in_=bparts[:, :, :], compare_op=ALU.is_equal, fill=0.0, base=-ROW_ADD,
                            pattern=[[-1, 3], [0, H]], channel_multiplier=1).then_inc(shaped, 1)
            g.affine_select(out=selv, in_=selv, compare_op=ALU.not_equal, fill=1.0, base=0,
                            pattern=[[-1, E], [0, 128]], channel_multiplier=1).then_inc(cleared, 1)
            pool.wait_ge(cleared, 5)
            g.affine_select(out=selv, in_=selv, compare_op=ALU.not_equal, fill=1.0, base=-32,
                            pattern=[[-1, E], [0, 128]], channel_multiplier=1).then_inc(shaped, 1)
            for n in ("K2", "K1"):
                g.memset(stack[n][:, :, :], 0.0).then_inc(cleared, 1)
            pool.wait_ge(cleared, 7)
            for n in ("K2", "K1"):
                g.memset(stack[n][ROW_ADD:ROW_ADD + 32, :, :], 1.0).then_inc(kset, 1)

            def split_parts(u, bt, following):
                for i, name in enumerate(("Q2", "K2", "Q1", "K1")):
                    wait_apart(pool, *read(u, name))
                    if i >= 2:
                        wait_apart(pool, stored[("Q2", "K2")[i - 2]], bt * 16 + 16)
                    elif following:
                        wait_apart(pool, stored[("Q1", "K1")[i]], bt * 16)
                    s, p, c = split[i % 2], parts[i % 2], bt * SPLIT_STEPS + 3 * i
                    g.tensor_scalar(p[:, 0, :], s[:, :], 1.0, None, ALU.mult).then_inc(pool_step, 1)
                    pool.wait_ge(pool_step, c + 1)
                    g.tensor_tensor(s[:, :], s[:, :], p[:, 0, :], ALU.subtract).then_inc(pool_step, 1)
                    wait_apart(pool, pool_step, c + 2)
                    g.tensor_scalar(p[:, 1, :], s[:, :], 1.0, None, ALU.mult).then_inc(pool_step, 1)
                    pool.wait_ge(pool_step, c + 3)
                    g.tensor_tensor(p[:, 2, :], s[:, :], p[:, 1, :], ALU.subtract).then_inc(parts_ready, 1)

            def mask(it):
                for hg in range(NG):
                    for q in range(4):
                        wait_apart(pool, weighed, it * NG * PIECES + hg * PIECES + q + 1)
                        v = PT[0][:, 896 * q:896 * q + 1024].rearrange("p (a n) -> p a n", n=512)[:, :, 0:128]
                        g.affine_select(out=v, in_=v, compare_op=ALU.is_ge, fill=0.0, base=0,
                                        pattern=[[0, 2], [1, 128]], channel_multiplier=-1).then_inc(masked, 1)
                    for q in range(2):
                        wait_apart(pool, weighed, it * NG * PIECES + hg * PIECES + 4 + q + 1)
                        v = PT[1][:, 768 * q:768 * q + 768].rearrange("p (r n) -> p r n", r=2)[:, :, 0:256]
                        g.affine_select(out=v, in_=v, compare_op=ALU.is_ge, fill=0.0, base=0,
                                        pattern=[[0, 2], [0, 2], [1, 128]], channel_multiplier=-1).then_inc(masked, 1)

            def weigh_experts(it):
                for e in range(1, NE):
                    k, c = score_use(it, 14 * NG + 2 * e + 1)
                    pool.wait_ge(s_read[k], c + 2)
                    k, c = acc_use(it, 2 * NG + 2 * e - 1)
                    pool.wait_ge(o_read[k], c + 2)
                    a = AB[e % 2].rearrange("p (f n) -> p f n", f=NFH)
                    w = CB[(e - 1) % 2].unsqueeze(1).broadcast_to([128, NFH, L])
                    g.tensor_tensor(a, a, w, ALU.mult).then_inc(routed, 1)

            pool.wait_ge(kset, 2)
            pool.wait_ge(setup, 1)
            split_parts(FIRST, 0, False)
            with pool.Fori(0, B - 1) as it:
                mask(it)
                split_parts(LOOP.row(it), it + 1, True)
                weigh_experts(it)
            mask(B - 1)
            weigh_experts(B - 1)

        @block.scalar
        def _(act):
            a = nc.scalar
            act.dma_start(PT[0][:, 0:NE * F].rearrange("p (e n) -> p e n", e=NE), w_gu[:, :, 0, :]).then_inc(gu_in, 16)
            act.dma_start(PT[1][:, 1024:1024 + NE * F].rearrange("p (e n) -> p e n", e=NE), w_gu[:, :, 1, :]).then_inc(gu_in, 16)
            act.dma_start(wdn[:, :, :, :], w_dn).then_inc(dn_in, 16)

            def tau():
                act.wait_ge(par_in, 16)
                a.activation(pt[0][:, :], pars[:, 0, :], ACT.Abs).then_inc(tau_step, 1)
                act.wait_ge(tau_step, 1)
                a.activation(pt[1][:, :], pt[0][:, :], ACT.Exp, scale=-1.0).then_inc(tau_step, 1)
                act.wait_ge(tau_step, 3)
                a.activation(pt[3][:, :], pt[2][:, :], ACT.Ln).then_inc(tau_step, 1)
                act.wait_ge(tau_step, 5)
                a.activation(pt[7][:, 0:H], pt[6][:, 0:H], ACT.Sigmoid).then_inc(tau_step, 1)

            def evacuate(u, name, dst, **scale):
                k, _n = u(name)
                act.wait_ge(*full(u, name))
                a.activation(dst, M[k][0:dst.shape[0], 0:dst.shape[-1]], ACT.Identity, **scale).then_inc(m_read[k], 1)

            def copy_v(u, name, V):
                k, _n = u(name)
                act.wait_ge(*full(u, name))
                a.activation(V[:, :, :, 0:HD], M[k][:, :].rearrange("p (t h d) -> p t h d", t=NT, h=H),
                             ACT.Copy).then_inc(m_read[k], 1)

            def root_norms(bt):
                act.wait_ge(roots_ready, bt + 1)
                a.activation(rinv[:, 0:2, :], root[:, 0:2, :], ACT.Sqrt).then_inc(rooted1, 1)

            def projections(u, bt, names):
                for name in names:
                    if name == "V2":
                        copy_v(u, name, V2)
                        continue
                    i = ("Q2", "K2", "Q1", "K1").index(name)
                    if i >= 2:
                        act.wait_ge(parts_ready, bt * 4 + i - 1)
                    scale = {"Q2": {"scale": HD ** -0.5}, "Q1": {"scale": qs1[:, :]}}.get(name, {})
                    evacuate(u, name, split[i % 2][:, :], **scale)

            def acc_out(it, G):
                k, _c = acc_use(it, G)
                act.wait_ge(pv_done, it * 4 * NG + 2 * G + 4)
                a.activation(OS[:, G % NG, :], O[k][:, :], ACT.Copy).then_inc(o_read[k], 1)

            def row(u, it, following):
                bt = it + 1
                for n in range(2 * NG):
                    act.wait_ge(pv_done, it * 4 * NG + n + 1)
                    if n == 0:
                        act.wait_ge(down_done, it * DOWNS + 2)
                    for q in range(4):
                        k, c = score_use(it, n * 4 + q)
                        act.wait_ge(s_full[k], c + 1)
                        a.activation(PT[n % 2][:, 1024 * q:1024 * q + 1024], S[k][:, :], ACT.Exp).then_inc(s_read[k], 1)
                    if n == 3:
                        evacuate(u, "maxT_Y", mTY[:, :])
                    if n % 2 == 0 and n > 0:
                        acc_out(it, n // 2 - 1)
                for hg in range(NG):
                    n = 2 * NG + 2 * hg
                    act.wait_ge(pv_done, it * 4 * NG + n + 1)
                    for q in range(4):
                        k, c = score_use(it, 8 * NG + hg * PIECES + q)
                        act.wait_ge(s_full[k], c + 1)
                        a.activation(PT[0][:, 896 * q:896 * q + 896], S[k][:, 0:896], ACT.Sigmoid).then_inc(s_read[k], 1)
                    if hg == 1:
                        act.wait_ge(*full(u, ("oT2", NT - 1)))
                    acc_out(it, NG - 1 + hg)
                    if hg == 2:
                        act.wait_ge(*read(u, "proj2"))
                        for t in range(NT):
                            a.activation(h2t[:, t, :], x1[:, t, :], ACT.Square, accum_out=ssum[:, t:t + 1]).then_inc(squared, 1)
                        if following:
                            root_norms(bt)
                        act.wait_ge(squared, (it + 1) * NT)
                        a.activation(rinv[:, 2, :], ssum[:, :], ACT.Sqrt, scale=1.0 / D, bias=eps6[:, :]).then_inc(rooted2, 1)
                    if hg == 3 and following:
                        projections(u, bt, ("Q2",))
                    act.wait_ge(pv_done, it * 4 * NG + n + 2)
                    for q in range(2):
                        k, c = score_use(it, 8 * NG + hg * PIECES + 4 + q)
                        act.wait_ge(s_full[k], c + 1)
                        a.activation(PT[1][:, 768 * q:768 * q + 768].rearrange("p (r n) -> p r n", r=2),
                                     S[k][:, :].rearrange("p (r n) -> p r n", r=2)[:, :, 0:384], ACT.Sigmoid).then_inc(s_read[k], 1)
                    if hg == 1:
                        evacuate(u, "ctxT2", ctxT[:, :])
                    if hg == 2:
                        evacuate(u, "h2T", h2T[:, :], scale=n2s[:, :])
                        if following:
                            evacuate(u, "xnT", xnT[:, :])
                            evacuate(u, "hT", hT[:, :], scale=n1s[:, :])
                    if hg == 3:
                        act.wait_ge(*read(u, "logits"))
                        a.activation(lp[:, :, :], ld[:, :, :], ACT.Sigmoid).then_inc(exps_ready, 1)
                        a.activation(lq[:, :, :], ld[:, :, :], ACT.Sigmoid, scale=-1.0).then_inc(exps_ready, 1)
                        if following:
                            projections(u, bt, ("K2", "V2", "Q1", "K1"))
                        act.wait_ge(gap_ready, it + 1)
                        a.activation(wtop[:, 0, :], dtop[:, :], ACT.Sigmoid).then_inc(top_ready, 1)
                        a.activation(wtop[:, 1, :], dtop[:, :], ACT.Sigmoid, scale=-1.0).then_inc(top_ready, 1)
                for e in range(NE):
                    k, c = score_use(it, 14 * NG + 2 * e)
                    act.wait_ge(s_full[k], c + 1)
                    act.wait_ge(down_done, it * DOWNS + e + 1)
                    if e == 0:
                        act.wait_ge(pv_done, it * 4 * NG + 4 * NG + 1)
                    a.activation(AB[e % 2], S[k][:, :], ACT.Silu).then_inc(s_read[k], 1)
                    if e == 0:
                        acc_out(it, 2 * NG - 1)
                    if e > 0:
                        k, c = acc_use(it, 2 * NG + 2 * e - 1)
                        act.wait_ge(cb_full, it * E + e)
                        act.wait_ge(routed, it * E + e)
                        a.activation(CB[(e - 1) % 2], O[k][:, :], ACT.Copy).then_inc(o_read[k], 1)
                    if e == 3:
                        evacuate(u, "ctxT1", ctxT[:, :])
                        if following:
                            copy_v(u, "V1", V1)
                    if e == 4:
                        evacuate(u, "proj1", sT[:, :])
                if following:
                    evacuate(u, "maxT_X", mTX[:, :])
                act.wait_ge(down_done, it * DOWNS + DOWNS + 2)
                a.activation(gT[:, :], O[0][:, :], ACT.Silu).then_inc(o_read[0], 1)

            root_norms(0)
            tau()
            act.wait_ge(w_in, 80)
            evacuate(FIRST, "xnT", xnT[:, :])
            evacuate(FIRST, "hT", hT[:, :], scale=n1s[:, :])
            act.wait_ge(setup, 1)
            projections(FIRST, 0, ("Q2", "K2", "V2", "Q1", "K1"))
            copy_v(FIRST, "V1", V1)
            evacuate(FIRST, "maxT_X", mTX[:, :])
            with act.Fori(0, B - 1) as it:
                row(LOOP.row(it), it, True)
            row(LAST, B - 1, False)

        @block.vector
        def _(dve):
            v = nc.vector
            steps = [0, 0]

            def step(ins, apart=False):
                ins.then_inc(dve_step, 1)
                steps[0] += 1
                if apart:
                    wait_apart(dve, dve_step, steps[1] + steps[0])
                else:
                    dve.wait_ge(dve_step, steps[1] + steps[0])

            def norm_stats(bt):
                dve.wait_ge(xin_in, bt * 16 + 16)
                for t in range(NT):
                    last = v.bn_stats(stats[:, t, :], xin[:, t, :])
                step(last, apart=True)
                for t in range(NT):
                    last = v.bn_aggr(mv[:, t, :], stats[:, t, :])
                step(last)
                v.tensor_scalar(root[:, 0, :], mv[:, :, 1], 1e-5, None, ALU.add)
                v.tensor_scalar(root[:, 1, :], mv[:, :, 1], 1.0 + 1e-6, 1e-11, ALU.mult, ALU.add).then_inc(roots_ready, 1)

            def norm_apply(bt):
                dve.wait_ge(rooted1, bt + 1)
                step(v.reciprocal(rinv[:, 0:2, :], rinv[:, 0:2, :]))
                for dst, i, ready in ((xn, 0, xn_ready), (ht, 1, h_ready)):
                    for t in range(NT):
                        last = v.tensor_scalar(dst[:, t, :], xin[:, t, :], mv[:, t, 0:1], rinv[:, i, t:t + 1],
                                               ALU.subtract, ALU.mult)
                    last.then_inc(ready, 1)

            def maxima(u, blocks):
                for h, t in blocks:
                    k, _n = u(("max", h, t))
                    dve.wait_ge(*full(u, ("max", h, t)))
                    v.tensor_reduce(nmax[:, h, t:t + 1], M[k][:, :], AX.X, ALU.max, negate=True).then_inc(m_read[k], 1)

            def maxima_parts(u, blocks, dst, ready):
                for b in blocks[-2:]:
                    dve.wait_ge(*read(u, ("max", *b)))
                h0, h1 = blocks[0][0], blocks[-1][0] + 1
                src = nmax[:, h0:h1, :].rearrange("p h t -> p (h t)")
                step(v.tensor_copy(dst[:, 0, :], src))
                v.tensor_tensor(dst[:, 1, :], src, dst[:, 0, :], ALU.subtract).then_inc(ready, 1)

            def attention_out(u, name, t):
                k, _n = u((name, t))
                w = M[k][:, :].rearrange("p (g q c) -> p (g q) c", g=NG, c=32)
                dve.wait_ge(*full(u, (name, t)))
                if name == "oT1":
                    step(v.tensor_tensor(dsum[:, t, :], w[:, :, HD], dcorr[:, t, :], ALU.add))
                    v.tensor_tensor(corr[:, t, :].rearrange("p (h d) -> p h d", h=H), w[:, :, 0:HD],
                                    corr[:, t, :].rearrange("p (h d) -> p h d", h=H), ALU.add).then_inc(m_read[k], 1)
                    step(v.reciprocal(rden[:, t, :], dsum[:, t, :]))
                    dve.wait_ge(*read(u, (name, t)))
                    v.tensor_tensor(ctxs[:, t, :].rearrange("p (h d) -> p h d", h=H),
                                    corr[:, t, :].rearrange("p (h d) -> p h d", h=H),
                                    rden[:, t, :].unsqueeze(2).broadcast_to([128, H, HD]), ALU.mult).then_inc(gated, 1)
                else:
                    step(v.reciprocal(rden[:, t, :], w[:, :, HD]))
                    v.tensor_tensor(ctxs[:, t, :].rearrange("p (h d) -> p h d", h=H), w[:, :, 0:HD],
                                    rden[:, t, :].unsqueeze(2).broadcast_to([128, H, HD]), ALU.mult).then_inc(m_read[k], 1)

            def weigh(it, hg, q):
                k, c = score_use(it, 8 * NG + hg * PIECES + q)
                dve.wait_ge(s_read[k], c + 2)
                p = PT[0][:, 896 * q:896 * q + 896] if q < 4 else PT[1][:, 768 * (q - 4):768 * (q - 4) + 768]
                v.scalar_tensor_tensor(p, p, 1.0, p, ALU.subtract, ALU.mult).then_inc(weighed, 1)

            def router(u, it):
                dve.wait_ge(exps_ready, 2 * it + 2)
                step(v.reciprocal(lq[:, :, :], lq[:, :, :]))
                step(v.tensor_tensor(lp[:, :, :], lp[:, :, :], lq[:, :, :], ALU.mult))
                step(v.tensor_reduce(lsum[:, :], lp[:, :, :], AX.X, ALU.add))
                step(v.reciprocal(lsum[:, :], lsum[:, :]))
                step(v.tensor_tensor(lp[:, :, :], lp[:, :, :], lsum[:, :].unsqueeze(2).broadcast_to([128, NT, E]), ALU.mult), apart=True)
                for t in range(NT):
                    last = v.max(top[:, t, :], lp[:, t, :])
                step(last)
                v.tensor_tensor(dtop[:, :], top[:, :, 0], top[:, :, 1], ALU.subtract).then_inc(gap_ready, 1)
                for t in range(NT):
                    last = v.max_index(topi[:, t, :], top[:, t, :], lp[:, t, :])
                step(last)
                step(v.tensor_copy(topf[:, :, :], topi[:, :, :]))

            def combine(it):
                dve.wait_ge(top_ready, 2 * it + 2)
                shape = [128, NT, E]
                for i, dst in ((0, lp), (1, lq)):
                    step(v.tensor_tensor(dst[:, :, :], iota_f[:, :].unsqueeze(1).broadcast_to(shape),
                                         topf[:, :, i:i + 1].broadcast_to(shape), ALU.is_equal))
                    step(v.tensor_tensor(dst[:, :, :], dst[:, :, :], wtop[:, i, :].unsqueeze(2).broadcast_to(shape), ALU.mult))
                v.tensor_tensor(comb[:, :, :], lp[:, :, :], lq[:, :, :], ALU.add).then_inc(comb_ready, 1)

            def row(u, it, following):
                bt = it + 1
                steps[0] = 0
                for n in range(3):
                    maxima(u, Y_AT[n])
                maxima_parts(u, MAX_Y, mhY, maxY_ready)
                if following:
                    norm_stats(bt)
                for hg in range(NG):
                    for q in range(4):
                        weigh(it, hg, q)
                    if hg == 0:
                        for t in range(NT):
                            attention_out(u, "oT2", t)
                    if hg == 2:
                        dve.wait_ge(rooted2, it + 1)
                        step(v.reciprocal(rinv[:, 2, :], rinv[:, 2, :]))
                        for t in range(NT):
                            last = v.tensor_scalar(h2t[:, t, :], x1[:, t, :], rinv[:, 2, t:t + 1], None, ALU.mult)
                        last.then_inc(h2_ready, 1)
                        if following:
                            norm_apply(bt)
                    for q in range(4, PIECES):
                        weigh(it, hg, q)
                    if hg == 1:
                        k, _n = u("proj2")
                        dve.wait_ge(*full(u, "proj2"))
                        v.tensor_tensor(x1[:, :, :].rearrange("p t d -> p (t d)"), M[k][:, :],
                                        xn[:, :, :].rearrange("p t d -> p (t d)"), ALU.add).then_inc(m_read[k], 1)
                    if hg == 2:
                        dve.wait_ge(*read(u, "h2T"))
                        step(v.tensor_copy(h2hi[:, :], h2T[:, :]))
                        v.tensor_tensor(h2lo[:, :], h2T[:, :], h2hi[:, :], ALU.subtract).then_inc(h2r_ready, 1)
                        k, _n = u("logits")
                        dve.wait_ge(*full(u, "logits"))
                        lg = M[k][:, 0:NT * E].rearrange("p (t e) -> p t e", t=NT)
                        step(v.tensor_reduce(lmax[:, :], lg, AX.X, ALU.max))
                        v.tensor_tensor(ld[:, :, :], lg, lmax[:, :].unsqueeze(2).broadcast_to([128, NT, E]),
                                        ALU.subtract).then_inc(m_read[k], 1)
                router(u, it)
                for e in range(NE):
                    k, c = score_use(it, 14 * NG + 2 * e)
                    k2, c2 = score_use(it, 14 * NG + 2 * e + 1)
                    dve.wait_ge(s_read[k], c + 2)
                    dve.wait_ge(s_full[k2], c2 + 1)
                    v.tensor_tensor(AB[e % 2], AB[e % 2], S[k2][:, :], ALU.mult).then_inc(s_read[k2], 1)
                    if e == 0:
                        combine(it)
                        k, _n = u("suffix")
                        dve.wait_ge(*full(u, "suffix"))
                        v.tensor_tensor(corr[:, :, :].rearrange("p t (h d) -> p t h d", h=H),
                                        M[k][:, :].rearrange("p (t h d) -> p t h d", t=NT, h=H),
                                        cneg[:, :].unsqueeze(1).unsqueeze(3).broadcast_to([128, NT, H, HD]),
                                        ALU.mult).then_inc(m_read[k], 1)
                        k, _n = u("combT")
                        dve.wait_ge(*full(u, "combT"))
                        step(v.tensor_copy(cT[0:E, :], M[k][0:E, :]))
                        v.tensor_tensor(cT[32:32 + E, :], M[k][0:E, :], cT[0:E, :], ALU.subtract).then_inc(m_read[k], 1)
                    if e == 1:
                        dve.wait_ge(*read(u, "suffix"))
                    if e in (1, 2):
                        for t in (2 * e - 2, 2 * e - 1):
                            attention_out(u, "oT1", t)
                    if following and e in X_AT:
                        maxima(u, X_AT[e])
                if following:
                    maxima_parts(u, MAX_X, mhX, maxX_ready)
                dve.wait_ge(o_read[0], it * O_USES[0] + O_USES[0] + 1)
                dve.wait_ge(*read(u, "proj1"))
                v.tensor_tensor(gT[:, :], gT[:, :], sT[:, :], ALU.mult).then_inc(prod_ready, 1)
                k, _n = u("outT")
                dve.wait_ge(*full(u, "outT"))
                dve.wait_ge(xres_in, it * 16 + 16)
                v.tensor_tensor(xres[:, :, :].rearrange("p t d -> p (t d)"), M[k][:, :],
                                xres[:, :, :].rearrange("p t d -> p (t d)"), ALU.add).then_inc(m_read[k], 1)
                assert steps[0] <= DVE_ROW and (not following or steps[0] == DVE_ROW)

            for k in range(2):
                v.memset(M[k][:, :], 0.0).then_inc(m_read[k], 1)
            norm_stats(0)
            norm_apply(0)
            for k in range(2):
                v.memset(S[k][:, :], 0.0).then_inc(s_read[k], 1)
                v.memset(O[k][:, :], 0.0).then_inc(o_read[k], 1)
            v.memset(eps6[:, :], 1e-6)
            v.memset(stack["Q2"][:, :, :].bitcast(dt.uint32), 0)
            v.memset(stack["Q1"][:, :, :].bitcast(dt.uint32), 0)
            v.memset(V1[:, :, :, :], 0.0)
            v.memset(V2[:, :, :, :], 0.0)
            step(v.memset(cT[:, :].bitcast(fp32), 0.0))
            v.memset(V1[:, :, :, HD:HD + 1], 1.0)
            v.memset(V2[:, :, :, HD:HD + 1], 1.0)
            dve.wait_ge(tau_step, 2)
            v.tensor_scalar(pt[2][:, :], pt[1][:, :], 1.0, None, ALU.add).then_inc(tau_step, 1)
            dve.wait_ge(tau_step, 4)
            step(v.tensor_scalar(pt[4][:, :], pt[2][:, :], -1.0, None, ALU.add))
            step(v.tensor_scalar(pt[5][:, :], pt[4][:, :], 0.0, None, ALU.is_equal))
            step(v.tensor_tensor(pt[6][:, :], pt[4][:, :], pt[5][:, :], ALU.add))
            step(v.reciprocal(pt[6][:, :], pt[6][:, :]))
            step(v.tensor_tensor(pt[6][:, :], pt[6][:, :], pt[3][:, :], ALU.mult))
            step(v.tensor_tensor(pt[6][:, :], pt[6][:, :], pt[5][:, :], ALU.add))
            step(v.tensor_tensor(pt[6][:, :], pt[6][:, :], pt[1][:, :], ALU.mult))
            step(v.scalar_tensor_tensor(pt[6][:, :], pars[:, 0, :], 0.0, pt[6][:, :], ALU.max, ALU.add))
            step(v.tensor_scalar(pt[6][:, :], pt[6][:, :], 1e-6, None, ALU.add))
            step(v.reciprocal(pt[5][:, :], pt[6][:, :]))
            step(v.tensor_scalar(pt[3][:, :], pt[5][:, :], 2.0, None, ALU.mult))
            v.tensor_scalar(qs1[:, :], pt[3][:, H:H + 1], HD ** -0.5, None, ALU.mult)
            step(v.scalar_tensor_tensor(pt[4][:, :], pars[:, 1, :], -1.0, pt[3][:, :], ALU.mult, ALU.mult))
            v.scalar_tensor_tensor(pt[6][:, :], pt[3][:, :], MASKED, pt[4][:, :], ALU.mult, ALU.add).then_inc(tau_step, 1)
            step(v.tensor_copy(bsplit[:, 0, :], pt[4][:, 0:H]))
            step(v.tensor_tensor(pt[5][:, 0:H], pt[4][:, 0:H], bsplit[:, 0, :], ALU.subtract))
            step(v.tensor_copy(bsplit[:, 1, :], pt[5][:, 0:H]))
            step(v.tensor_tensor(bsplit[:, 2, :], pt[5][:, 0:H], bsplit[:, 1, :], ALU.subtract))
            dve.wait_ge(shaped, 5)
            step(v.tensor_tensor(bparts[:, :, :], bparts[:, :, :], bsplit[:, :, :], ALU.mult))
            step(v.tensor_reduce(brow[:, :], bparts[:, :, :].rearrange("p a h -> p h a"), AX.X, ALU.add))
            step(v.tensor_copy(stack["Q1"][ROW_ADD:ROW_ADD + 32, :, :],
                               brow[ROW_ADD:ROW_ADD + 32, :].unsqueeze(2).broadcast_to([32, H, L])))
            dve.wait_ge(counted, 2)
            v.tensor_copy(iota_f[:, :], iota_i[:, :])
            step(v.tensor_copy(rest_f[:, :], rest_i[:, :]))
            dve.wait_ge(tau_step, 6)
            step(v.scalar_tensor_tensor(cneg[:, :], pt[7][:, 0:H], 1.0, pt[7][:, 0:H], ALU.subtract, ALU.mult))
            step(v.tensor_tensor(dcorr[:, :, :], rest_f[:, :].unsqueeze(2).broadcast_to([128, NT, H]),
                                 cneg[:, :].unsqueeze(1).broadcast_to([128, NT, H]), ALU.mult))
            step(v.tensor_scalar(dcorr[:, :, :], dcorr[:, :, :], -2.5e-7, None, ALU.add))
            step(v.tensor_copy(identb[:, :], ident[:, :]))
            v.tensor_copy(sel[:, :, :], PT[1][:, 0:E * 128].rearrange("p (e m) -> p e m", e=E)).then_inc(setup, 1)
            dve.wait_ge(gu_in, 32)
            for i, src in enumerate((PT[0][:, 0:NE * F], PT[1][:, 1024:1024 + NE * F])):
                src = src.rearrange("p (e n) -> p e n", e=NE)
                step(v.tensor_copy(wgu_hi[:, :, i * F:i * F + F], src))
                last = v.tensor_tensor(wgu_lo[:, :, i * F:i * F + F], src, wgu_hi[:, :, i * F:i * F + F], ALU.subtract)
            last.then_inc(pv_done, 2)
            dve.sem_inc(routed, 2)
            dve.sem_inc(down_done, 2)
            for e in X_AT:
                maxima(FIRST, X_AT[e])
            maxima_parts(FIRST, MAX_X, mhX, maxX_ready)
            assert steps[0] == DVE_FIRST
            steps[1] = DVE_FIRST
            with dve.Fori(0, B - 1) as it:
                steps[1] = DVE_FIRST + it * DVE_ROW
                row(LOOP.row(it), it, True)
            steps[1] = DVE_FIRST + (B - 1) * DVE_ROW
            row(LAST, B - 1, False)

        @block.tensor
        def _(pe):
            t_ = nc.tensor
            order = []

            def begin(u, name):
                order.append(name)
                assert u.order[len(order) - 1] == name, (name, u.order[len(order) - 1])
                k, _n = u(name)
                pe.wait_ge(*free(u, name))
                return k

            def transposed(u, name, src):
                k = begin(u, name)
                for t in range(NT):
                    last = t_.transpose(M[k][:, t * 128:t * 128 + 128], src[:, t, :], ident[:, :])
                last.then_inc(m_full[k], 1)

            def projected(u, name, w, src):
                k = begin(u, name)
                t_.matmul(M[k][:, :], w, src[:, :], start=True, stop=True).then_inc(m_full[k], 1)

            def projected_v(u, name, w, src):
                k = begin(u, name)
                for t in range(NT):
                    last = t_.matmul(M[k][:, t * 128:t * 128 + 128], src[:, t * 128:t * 128 + 128], w, start=True, stop=True)
                last.then_inc(m_full[k], 1)

            def maxima(u, blocks):
                for h, t in blocks:
                    k = begin(u, ("max", h, t))
                    t_.matmul(M[k][:, :], stack["Q2"][0:ROW_ADD, h, t * 128:t * 128 + 128], stack["K2"][0:ROW_ADD, h, :],
                              start=True, stop=True).then_inc(m_full[k], 1)

            def maxima_T(u, name, src, ready, n):
                pe.wait_ge(ready, n + 1)
                k = begin(u, name)
                t_.matmul(M[k][0:src.shape[1] * src.shape[2], 0:128], src[:, :, :], identb[:, :], start=True, stop=True)\
                    .then_inc(m_full[k], 1)

            def out_T(u, name, t):
                k = begin(u, (name, t))
                for hg in range(NG):
                    last = t_.transpose(M[k][:, hg * 128:hg * 128 + 128], OS[:, hg, t * 128:t * 128 + 128], ident[:, :])
                last.then_inc(m_full[k], 1)

            def scores(it, n, q):
                if n < 2 * NG:
                    k, c = score_use(it, 4 * n + q)
                    pe.wait_ge(s_read[k], c + 1)
                    h = 4 * (n // 2) + q
                    for j in range(2):
                        jb = 2 * (n % 2) + j
                        last = t_.matmul(S[k][:, j * 512:j * 512 + 512], stack["K2"][:, h, jb * 128:jb * 128 + 128],
                                         stack["Q2"][:, h, :], start=True, stop=True)
                    last.then_inc(s_full[k], 1)
                    return
                hg, late = (n - 2 * NG) // 2, n % 2
                k, c = score_use(it, 8 * NG + hg * PIECES + 4 * late + q)
                pe.wait_ge(s_read[k], c + 1)
                for j in range(4):
                    if late:
                        h, jb, at = 4 * hg + 2 * q + j // 2, 3 - j % 2, 512 * (j // 2) + 128 * (j % 2)
                    elif j < 2:
                        h, jb, at = 4 * hg + q, j, 512 * j
                    else:
                        break
                    i0 = jb * 128
                    last = t_.matmul(S[k][:, at:at + L - i0], stack["K1"][:, h, i0:i0 + 128], stack["Q1"][:, h, i0:L],
                                     start=True, stop=True)
                last.then_inc(s_full[k], 1)

            def with_v(it, n, half):
                G, late = n // 2, n % 2
                jb = 2 * late + half
                if late == 0 and half == 0:
                    k, c = acc_use(it, G)
                    pe.wait_ge(o_read[k], c + 1)
                if half == 0:
                    if n < 2 * NG:
                        for k in range(2):
                            pe.wait_ge(s_read[k], it * S_USES + 2 * n + 2 + 1)
                    else:
                        pe.wait_ge(masked, it * NG * PIECES + (G - NG) * PIECES + (PIECES if late else 4))
                for q in range(4):
                    if n < 2 * NG:
                        V, i0, at = V2, 0, 1024 * q + 512 * half
                    elif late:
                        V, i0, at = V1, jb * 128, 384 * q + 128 * (1 - half)
                    else:
                        V, i0, at = V1, jb * 128, 896 * q + 512 * half
                    last = t_.matmul(O[G % 2][32 * q:32 * q + VW, i0:L], V[:, jb, 4 * (G % NG) + q, :],
                                     PT[late][:, at:at + L - i0], start=(jb == 0), stop=(jb == NT - 1))
                if half:
                    last.then_inc(pv_done, 1)

            def first_products(it, e):
                for i in range(2):
                    k, c = score_use(it, 14 * NG + 2 * e + i)
                    pe.wait_ge(s_read[k], c + 1)
                    for f in range(NFH):
                        cols = slice(i * F + f * 128, i * F + f * 128 + 128)
                        dst = S[k][:, f * 512:f * 512 + 512]
                        t_.matmul(dst, wgu_hi[:, e, cols], h2hi[:, :], start=True, stop=False)
                        t_.matmul(dst, wgu_hi[:, e, cols], h2lo[:, :], start=False, stop=False)
                        last = t_.matmul(dst, wgu_lo[:, e, cols], h2hi[:, :], start=False, stop=True)
                    last.then_inc(s_full[k], 1)

            def routing_weights(u, it, e):
                k, c = acc_use(it, 2 * NG + 2 * e - 1)
                pe.wait_ge(o_read[k], c + 1)
                if e == 1:
                    pe.wait_ge(*read(u, "combT"))
                t_.matmul(O[k][:, :], sel[:, e - 1, :], cT[:, :], start=True, stop=True).then_inc(cb_full, 1)

            def second_product(it, e):
                if e == 0:
                    pe.wait_ge(o_read[0], it * O_USES[0] + NG + 1)
                    k, c = score_use(it, 14 * NG + 1)
                    pe.wait_ge(s_read[k], c + 2)
                else:
                    pe.wait_ge(routed, it * E + e + 2)
                for f in range(NFH):
                    last = t_.matmul(O[0][:, :], wdn[:, e, f, :], AB[e % 2][:, f * 512:f * 512 + 512],
                                     start=(e == 0 and f == 0), stop=False)
                last.then_inc(down_done, 1)

            def row(u, it, following):
                bt = it + 1
                order.clear()
                pe.wait_ge(rowX, (it + 1) * 32)
                for n in range(2 * NG):
                    if n == 2 * (HX // 4):
                        pe.wait_ge(rowY, (it + 1) * 32)
                    scores(it, n, 0)
                    scores(it, n, 1)
                    if n:
                        with_v(it, n - 1, 0)
                    scores(it, n, 2)
                    if n:
                        with_v(it, n - 1, 1)
                    scores(it, n, 3)
                    if n in Y_AT:
                        maxima(u, Y_AT[n])
                    if n == 3:
                        maxima_T(u, "maxT_Y", mhY, maxY_ready, it)
                for name in ("Q1", "K1"):
                    pe.wait_ge(stacked[name], (it + 1) * 16 * len(PAIRS))
                for n in range(2 * NG, 4 * NG):
                    late = n % 2
                    scores(it, n, 0)
                    if not late:
                        scores(it, n, 1)
                    with_v(it, n - 1, 0)
                    if not late:
                        scores(it, n, 2)
                    else:
                        scores(it, n, 1)
                    with_v(it, n - 1, 1)
                    if not late:
                        scores(it, n, 3)
                    if n == 9:
                        pe.wait_ge(o_read[0], it * O_USES[0] + 3)
                        pe.wait_ge(o_read[1], it * O_USES[1] + 3)
                        for t in range(NT):
                            out_T(u, "oT2", t)
                    if n == 10:
                        pe.wait_ge(*read(u, ("oT2", NT - 2)))
                        pe.wait_ge(*read(u, ("oT2", NT - 1)))
                        transposed(u, "ctxT2", ctxs)
                    if n == 11:
                        pe.wait_ge(*read(u, "ctxT2"))
                        projected_v(u, "proj2", w2s[:, 3, :], ctxT)
                    if n == 13:
                        pe.wait_ge(h2_ready, it + 1)
                        transposed(u, "h2T", h2t)
                        if following:
                            pe.wait_ge(xn_ready, bt + 1)
                            transposed(u, "xnT", xn)
                            pe.wait_ge(h_ready, bt + 1)
                            transposed(u, "hT", ht)
                        pe.wait_ge(*read(u, "h2T"))
                        k = begin(u, "logits")
                        for t in range(NT):
                            last = t_.matmul(M[k][:, t * E:t * E + E], h2T[:, t * 128:t * 128 + 128], rts[:, :], start=True, stop=True)
                        last.then_inc(m_full[k], 1)
                    if n == 14 and following:
                        projections(u, ("Q2",))
                    if n == 15 and following:
                        projections(u, ("K2", "V2", "Q1", "K1"))
                pe.wait_ge(h2r_ready, it + 1)
                for e in range(NE):
                    first_products(it, e)
                    if e == 0:
                        with_v(it, 4 * NG - 1, 0)
                        with_v(it, 4 * NG - 1, 1)
                        k = begin(u, "suffix")
                        for t in range(NT):
                            for j in range(t, NT):
                                last = t_.matmul(M[k][:, t * 128:t * 128 + 128], (below if j == t else ones)[:, :],
                                                 V1[:, j, :, 0:HD], start=(j == t), stop=(j == NT - 1))
                        last.then_inc(m_full[k], 1)
                        pe.wait_ge(comb_ready, it + 1)
                        k = begin(u, "combT")
                        for t in range(NT):
                            last = t_.matmul(M[k][0:E, t * 128:t * 128 + 128], comb[:, t, :], ident[:, :], start=True, stop=True)
                        last.then_inc(m_full[k], 1)
                    else:
                        routing_weights(u, it, e)
                        second_product(it, e - 1)
                    if e == 0:
                        pe.wait_ge(o_read[0], it * O_USES[0] + NG + 1)
                        pe.wait_ge(o_read[1], it * O_USES[1] + NG + 1)
                        for t in range(2):
                            out_T(u, "oT1", t)
                    if e == 1:
                        if following:
                            for name in ("Q2", "K2"):
                                pe.wait_ge(stacked[name], (bt + 1) * 16 * len(PAIRS))
                            maxima(u, X_AT[e])
                        for t in range(2, NT):
                            out_T(u, "oT1", t)
                    elif e == 2:
                        if following:
                            maxima(u, X_AT[e])
                        pe.wait_ge(gated, (it + 1) * NT)
                        transposed(u, "ctxT1", ctxs)
                    elif e == 3:
                        if following:
                            projected_v(u, "V1", w1s[:, 2, :], xnT)
                            maxima(u, X_AT[e])
                        pe.wait_ge(*read(u, "ctxT1"))
                        projected(u, "proj1", w1s[:, 3, :], ctxT)
                    elif following and e in X_AT:
                        maxima(u, X_AT[e])
                second_product(it, NE - 1)
                if following:
                    maxima_T(u, "maxT_X", mhX, maxX_ready, bt)
                for t in range(NT):
                    last = t_.matmul(O[0][:, t * 128:t * 128 + 128], x1[:, t, :], ident[:, :], start=False, stop=(t == NT - 1))
                last.then_inc(down_done, 1)
                pe.wait_ge(prod_ready, it + 1)
                k = begin(u, "outT")
                for t in range(NT):
                    last = t_.transpose(M[k][:, t * 128:t * 128 + 128], gT[:, t * 128:t * 128 + 128], ident[:, :])
                last.then_inc(m_full[k], 1)
                assert len(order) == len(u.order)

            def projections(u, names):
                for name in names:
                    if name == "V2":
                        projected_v(u, name, w2s[:, 2, :], hT)
                    else:
                        w, src = (w2s, hT) if name[1] == "2" else (w1s, xnT)
                        projected(u, name, w[:, 0 if name[0] == "Q" else 1, :], src)

            pe.wait_ge(shaped, 5)
            pe.wait_ge(w_in, 80)
            pe.wait_ge(xn_ready, 1)
            transposed(FIRST, "xnT", xn)
            pe.wait_ge(h_ready, 1)
            transposed(FIRST, "hT", ht)
            pe.wait_ge(*read(FIRST, "xnT"))
            pe.wait_ge(*read(FIRST, "hT"))
            projections(FIRST, ("Q2", "K2", "V2", "Q1", "K1"))
            for name in ("Q2", "K2"):
                pe.wait_ge(stacked[name], 16 * len(PAIRS))
            for e in range(1, 3):
                maxima(FIRST, X_AT[e])
            projected_v(FIRST, "V1", w1s[:, 2, :], xnT)
            for e in range(3, 8):
                maxima(FIRST, X_AT[e])
            maxima_T(FIRST, "maxT_X", mhX, maxX_ready, 0)
            pe.wait_ge(dn_in, 16)
            with pe.Fori(0, B - 1) as it:
                row(LOOP.row(it), it, True)
            row(LAST, B - 1, False)


_INS = ["x", "par", "n1w", "n2w", "w1", "w2", "router", "w_gu", "w_dn"]


def kernel(L0_attn_x, L0_attn_Wq, L0_attn_Wk, L0_attn_Wv, L0_attn_Wo, L0_attn_compressibility, L0_attn_phase_threshold,
           L0_ffn_norm1_w, L0_ffn_norm2_w, L0_ffn_wq, L0_ffn_wk, L0_ffn_wv, L0_ffn_wo, L0_ffn_router_w,
           L0_ffn_sh_gate, L0_ffn_sh_up, L0_ffn_sh_down, L0_ffn_e_gate, L0_ffn_e_up, L0_ffn_e_down):
    import numpy as np
    import concourse.bacc as bacc
    from concourse import mybir as mb
    from concourse.bass_utils import run_bass_kernel_spmd

    def per_head(v):
        v = np.asarray(v).reshape(H)
        return np.concatenate([np.broadcast_to(v, (128, H)), np.repeat(v, HD)[:, None]], axis=1)

    gate = np.concatenate([np.asarray(L0_ffn_sh_gate)[None], np.asarray(L0_ffn_e_gate)])
    up = np.concatenate([np.asarray(L0_ffn_sh_up)[None], np.asarray(L0_ffn_e_up)])
    down = np.concatenate([np.asarray(L0_ffn_sh_down)[None], np.asarray(L0_ffn_e_down)])
    arrays = {
        "x": np.asarray(L0_attn_x),
        "par": np.stack([per_head(L0_attn_compressibility), per_head(L0_attn_phase_threshold)], axis=1),
        "n1w": np.asarray(L0_ffn_norm1_w)[:, None],
        "n2w": np.asarray(L0_ffn_norm2_w)[:, None],
        "w1": np.stack([np.asarray(w).T for w in (L0_attn_Wq, L0_attn_Wk, L0_attn_Wv, L0_attn_Wo)], axis=1),
        "w2": np.stack([np.asarray(w) for w in (L0_ffn_wq, L0_ffn_wk, L0_ffn_wv, L0_ffn_wo)], axis=1),
        "router": np.asarray(L0_ffn_router_w),
        "w_gu": np.stack([gate, up], axis=1).transpose(2, 0, 1, 3),
        "w_dn": down.reshape(NE, NFH, 128, D).transpose(2, 0, 1, 3),
    }
    arrays = {n: np.ascontiguousarray(a) for n, a in arrays.items()}
    nc = bacc.Bacc("TRN2", target_bir_lowering=False, num_devices=1)
    args = [nc.dram_tensor("in_" + n, arrays[n].shape, mb.dt.from_np(arrays[n].dtype), kind="ExternalInput").ap() for n in _INS]
    out = nc.dram_tensor("out_0", (B, L, D), mb.dt.float32, kind="ExternalOutput").ap()
    program(nc, *args, out)
    r = run_bass_kernel_spmd(nc, [{"in_" + n: arrays[n] for n in _INS}], core_ids=[0])
    return r.results[0]["out_0"]
```

```python
import concourse.bass as bass
from concourse import mybir
from contextlib import ExitStack

B, L, D = 8, 512, 128
H, HD = 16, 8
E, F = 8, 256
NE = E + 1
NT = L // 128
NG = H // 4
VW = 12
NFH = F // 128
PAIRS = [(0, 0), (0, 1), (0, 2), (1, 0), (1, 1), (2, 0)]
ROW_ADD = 64
HX = 12
MASKED = -10000.0

STAGE1 = [(g, "all", [j]) for g in range(NG) for j in range(NT)]
STAGE2 = [(g, kind, js) for g in range(NG) for kind, js in (("first", [0]), ("second", [1]), ("rest", [3, 2]))]
ATTENTION = STAGE1 + STAGE2
N1, UNITS = len(STAGE1), len(ATTENTION)
SLOTS = 4


def width(n):
    _g, kind, js = ATTENTION[n]
    return L if kind == "all" else sum(L - 128 * j for j in js)


MAX_Y = [("max", h, t) for h in range(HX, H) for t in range(NT)]
MAX_X = [("max", h, t) for h in range(HX) for t in range(NT)]
EXPERT, END = UNITS, UNITS + NE
PLACES = {n: [] for n in range(END + 1)}
for _n in range(8):
    PLACES[_n] += MAX_Y[2 * _n:2 * _n + 2]
PLACES[9] += ["maxT_Y"]
PLACES[18] += ["xnT", "hT"]
PLACES[19] += ["Q2"]
PLACES[20] += ["K2", ("oT2", 0)]
PLACES[21] += [("oT2", 1), ("oT2", 2)]
PLACES[22] += [("oT2", 3), "V2"]
PLACES[23] += ["ctxT2"]
PLACES[24] += ["proj2"]
PLACES[27] += ["h2T"]
PLACES[EXPERT] += ["logits", "Q1", "suffix"]
PLACES[EXPERT + 1] += ["K1", "combT"]
PLACES[EXPERT + 2] += [("oT1", 0), ("oT1", 1)]
PLACES[EXPERT + 3] += [("oT1", 2), ("oT1", 3)]
PLACES[EXPERT + 4] += ["V1", "ctxT1"]
PLACES[EXPERT + 5] += ["proj1"]
_at = 0
for _e, _count in ((1, 3), (2, 6), (3, 6), (4, 7), (5, 7), (6, 7), (7, 7), (8, 5)):
    PLACES[EXPERT + _e] += MAX_X[_at:_at + _count]
    _at += _count
PLACES[END - 1] += ["maxT_X"]
PLACES[END] += ["outT"]
AHEAD = {"xnT", "hT", "Q2", "K2", "V2", "Q1", "K1", "V1", "maxT_X", *MAX_X}


class Uses:

    def __init__(self, own, following, before=(0, 0)):
        self.places = {n: [w for w in work if (following if w in AHEAD else own)] for n, work in PLACES.items()}
        self.order = [w for n in sorted(self.places) for w in self.places[n]]
        self.at = {name: n for n, name in enumerate(self.order)}
        self.total = [(len(self.order) + 1) // 2, len(self.order) // 2]
        self.before = before

    def __call__(self, name):
        n = self.at[name]
        return n % 2, self.before[n % 2] + n // 2

    def row(self, it):
        later = Uses.__new__(Uses)
        later.places, later.order, later.at, later.total = self.places, self.order, self.at, self.total
        later.before = tuple(b + it * t for b, t in zip(self.before, self.total))
        return later


FIRST = Uses(False, True)
LOOP = Uses(True, True, FIRST.total)
LAST = Uses(True, False, LOOP.row(B - 1).before)

S_USES = UNITS + NE
O_USES = (2 * NG // 2 + 1, 2 * NG // 2 + E)
WEIGHED = 2 * len(STAGE2)
DOWNS = NE + 1
DEPTH = 3
DVE_FIRST, DVE_ROW = 31, 34
SPLIT_STEPS = 8


def program(nc, x, par, n1w, n2w, w1, w2, router, w_gu, w_dn, out):
    dt, ALU, ACT, AX = mybir.dt, mybir.AluOpType, mybir.ActivationFunctionType, mybir.AxisListType
    fp32, fp32r, bf16 = dt.float32, dt.float32r, dt.bfloat16

    ctx_ = ExitStack()
    with ctx_:
        def sb(name, shape, t=fp32):
            return ctx_.enter_context(nc.sbuf_tensor(name, shape, t))

        def sem(name):
            return ctx_.enter_context(nc.semaphore(name))

        xin = sb("xin", [128, NT, D])
        xres = sb("xres", [128, NT, D])
        xn = sb("xn", [128, NT, D])
        ht = sb("ht", [128, NT, D])
        x1 = sb("x1", [128, NT, D])
        h2t = sb("h2t", [128, NT, D])
        ctxs = ht
        ctxT = sb("ctxT", [128, L])
        xnT = sb("xnT", [128, L])
        hT = sb("hT", [128, L])
        h2T = sb("h2T", [128, L])
        h2hi = sb("h2hi", [128, L], fp32r)
        h2lo = sb("h2lo", [128, L], fp32r)
        sT = sb("sT", [128, L])
        gT = h2T
        corr = h2T[:, :].rearrange("p (t d) -> p t d", t=NT)
        split = [sb(f"split{i}", [128, L]) for i in range(2)]
        parts = [sb(f"parts{i}", [128, 3, L], bf16) for i in range(2)]
        stack = {n: sb("stack" + n, [128, H, L], bf16) for n in ("Q2", "K2", "Q1", "K1")}
        V2 = sb("V2", [128, NT, H, VW])
        V1 = sb("V1", [128, NT, H, VW])
        PT = sb("PT", [128, SLOTS, 4 * L])
        AB = [PT[:, i, 0:NFH * L] for i in range(DEPTH)]
        CB = [PT[:, i, NFH * L:NFH * L + L] for i in range(DEPTH)]
        OS = sb("OS", [128, NG, L])
        cT = sb("cT", [128, L], fp32r)
        wgu_hi = sb("wgu_hi", [128, NE, 2 * F], fp32r)
        wgu_lo = sb("wgu_lo", [128, NE, 2 * F], fp32r)
        wdn = sb("wdn", [128, NE, NFH, D])
        w1s = sb("w1s", [128, 4, D])
        w2s = sb("w2s", [128, 4, D])
        rts = sb("rts", [128, E])
        n1s = sb("n1s", [128, 1])
        n2s = sb("n2s", [128, 1])
        ident = sb("ident", [128, 128])
        identb = sb("identb", [128, 128], bf16)
        below = sb("below", [128, 128])
        ones = sb("ones", [128, 128])
        sel = sb("sel", [128, E, 128], fp32r)
        nmax = sb("nmax", [128, H, NT])
        mhX = sb("mhX", [128, 2, HX * NT], bf16)
        mhY = sb("mhY", [128, 2, (H - HX) * NT], bf16)
        mTX = sb("mTX", [2 * HX * NT, 128], bf16)
        mTY = sb("mTY", [2 * (H - HX) * NT, 128], bf16)
        stats = sb("stats", [128, NT, 6])
        mv = sb("mv", [128, NT, 2])
        root = sb("root", [128, 3, NT])
        rinv = sb("rinv", [128, 3, NT])
        eps6 = sb("eps6", [128, 1])
        ssum = sb("ssum", [128, NT])
        rden = sb("rden", [128, NT, H])
        dsum = sb("dsum", [128, NT, H])
        dcorr = sb("dcorr", [128, NT, H])
        cneg = sb("cneg", [128, H])
        qs1 = sb("qs1", [128, 1])
        pars = sb("pars", [128, 2, H + 1])
        pt = [sb(f"pt{i}", [128, H + 1]) for i in range(8)]
        bparts = sb("bparts", [128, 3, H])
        bsplit = sb("bsplit", [128, 3, H], bf16)
        brow = sb("brow", [128, H])
        iota_i = sb("iota_i", [128, E], dt.int32)
        rest_i = sb("rest_i", [128, NT], dt.int32)
        iota_f = sb("iota_f", [128, E])
        rest_f = sb("rest_f", [128, NT])
        lmax = sb("lmax", [128, NT])
        ld = sb("ld", [128, NT, E])
        lp = sb("lp", [128, NT, E])
        lq = sb("lq", [128, NT, E])
        lsum = sb("lsum", [128, NT])
        wgap = sb("wgap", [128, NT])
        top = sb("top", [128, NT, 8])
        topi = sb("topi", [128, NT, 8], dt.uint32)
        topf = sb("topf", [128, NT, 8])
        dtop = sb("dtop", [128, NT])
        wtop = sb("wtop", [128, 2, NT])
        comb = sb("comb", [128, NT, E])
        scratch = {n: nc.dram_tensor("scr" + n, [3, 128, L], bf16).ap() for n in stack}

        def pb(name, cols):
            return ctx_.enter_context(nc.psum_tensor(name, [128, cols], fp32))

        S = [pb("S0", 1024), pb("S1", 1024)]
        O = [pb("O0", 512), pb("O1", 512)]
        M = [pb("M0", 512), pb("M1", 512)]

        s_full, s_read = [sem("s_full0"), sem("s_full1")], [sem("s_read0"), sem("s_read1")]
        m_full, m_read = [sem("m_full0"), sem("m_full1")], [sem("m_read0"), sem("m_read1")]
        o_read = [sem("o_read0"), sem("o_read1")]
        pv_done = sem("pv_done")
        weighed = sem("weighed")
        masked = sem("masked")
        cb_full = sem("cb_full")
        routed = sem("routed")
        down_done = sem("down_done")
        xn_ready, h_ready, h2_ready, h2r_ready = (sem(n) for n in ("xn_ready", "h_ready", "h2_ready", "h2r_ready"))
        roots_ready, rooted1, rooted2, squared = (sem(n) for n in ("roots_ready", "rooted1", "rooted2", "squared"))
        exps_ready, gap_ready, top_ready, comb_ready = (sem(n) for n in ("exps_ready", "gap_ready", "top_ready", "comb_ready"))
        parts_ready, maxX_ready, maxY_ready, prod_ready = (sem(n) for n in ("parts_ready", "maxX_ready", "maxY_ready", "prod_ready"))
        stored = {n: sem("stored" + n) for n in stack}
        stacked = {n: sem("stacked" + n) for n in stack}
        rowX, rowY = sem("rowX"), sem("rowY")
        xin_in, xres_in, written = sem("xin_in"), sem("xres_in"), sem("written")
        par_in, w_in, gu_in, dn_in = sem("par_in"), sem("w_in"), sem("gu_in"), sem("dn_in")
        dve_step, pool_step = sem("dve_step"), sem("pool_step")
        passed = sem("passed")
        carried = sem("carried")
        gated = sem("gated")
        cleared, shaped, counted, kset, setup, tau_step = (
            sem(n) for n in ("cleared", "shaped", "counted", "kset", "setup", "tau_step"))

        x_t = x.rearrange("b (t p) d -> b p t d", p=128)
        out_t = out.rearrange("b (t p) d -> b p t d", p=128)
        block = ctx_.enter_context(nc.Block())

        def full(u, name):
            k, n = u(name)
            return m_full[k], n + 1

        def read(u, name):
            k, n = u(name)
            return m_read[k], n + 2

        def free(u, name):
            k, n = u(name)
            return m_read[k], n + 1

        def wait_apart(engine, semaphore, value):
            engine.wait_ge(semaphore, value)
            engine.sem_inc(passed, 1)

        def score_use(it, n):
            return n % 2, it * S_USES + n // 2

        def acc_use(it, G):
            return G % 2, it * O_USES[G % 2] + G // 2

        @block.sync
        def _(sp):
            sp.dma_start(xin[:, :, :], x_t[0]).then_inc(xin_in, 16)
            sp.dma_start(pars[:, :, :], par).then_inc(par_in, 16)
            sp.dma_start(n1s[:, :], n1w).then_inc(w_in, 16)
            sp.dma_start(n2s[:, :], n2w).then_inc(w_in, 16)
            sp.dma_start(w2s[:, :, :], w2).then_inc(w_in, 16)
            sp.dma_start(w1s[:, :, :], w1).then_inc(w_in, 16)
            sp.dma_start(rts[:, :], router).then_inc(w_in, 16)

            def restack(name, i, bt):
                sp.wait_ge(parts_ready, bt * 4 + i + 1)
                sp.dma_start(scratch[name].rearrange("a p n -> p a n"), parts[i % 2][:, :, :]).then_inc(stored[name], 16)
                sp.wait_ge(stored[name], bt * 16 + 16)
                side = 0 if name[0] == "Q" else 1
                for c, pair in enumerate(PAIRS):
                    sp.dma_start(stack[name][HD * c:HD * c + HD, :, :],
                                 scratch[name][pair[side]].rearrange("(h d) n -> d h n", d=HD)).then_inc(stacked[name], 16)

            def maxima_rows(mT, rows, h0, h1):
                per = (h1 - h0) * NT
                for part in range(2):
                    row = stack["Q2"][ROW_ADD + part:ROW_ADD + part + 1, h0:h1, :]
                    sp.dma_start(row.rearrange("o h (t n) -> o (h t) n", n=128),
                                 mT[part * per:(part + 1) * per, :]).then_inc(rows, 16)

            def prepare(u, bt, it=None):
                for i, name in enumerate(("Q2", "K2")):
                    if it is not None:
                        for k in range(2):
                            wait_apart(sp, s_full[k], it * S_USES + N1)
                    restack(name, i, bt)
                for i, name in enumerate(("Q1", "K1")):
                    if it is not None:
                        for k in range(2):
                            wait_apart(sp, s_full[k], it * S_USES + UNITS)
                    restack(name, i + 2, bt)
                wait_apart(sp, *read(u, "maxT_X"))
                maxima_rows(mTX, rowX, 0, HX)

            def row(u, it, following):
                if following:
                    wait_apart(sp, h_ready, it + 1)
                    sp.dma_start(xin[:, :, :], x_t[bass.ds(it + 1, 1)].rearrange("o p t d -> (o p) t d")).then_inc(xin_in, 16)
                sp.dma_start(xres[:, :, :], x_t[bass.ds(it, 1)].rearrange("o p t d -> (o p) t d")).then_inc(xres_in, 16)
                wait_apart(sp, *read(u, "maxT_Y"))
                maxima_rows(mTY, rowY, HX, H)
                if following:
                    prepare(u, it + 1, it)
                wait_apart(sp, *read(u, "outT"))
                sp.dma_start(out_t[bass.ds(it, 1)].rearrange("o p t d -> (o p) t d"), xres[:, :, :]).then_inc(written, 16)
                wait_apart(sp, written, it * 16 + 16)

            sp.wait_ge(kset, 2)
            sp.wait_ge(setup, 1)
            prepare(FIRST, 0)
            with sp.Fori(0, B - 1) as it:
                row(LOOP.row(it), it, True)
            row(LAST, B - 1, False)

        @block.gpsimd
        def _(pool):
            g = nc.gpsimd
            g.memset(ident[:, :], 0.0).then_inc(cleared, 1)
            g.memset(below[:, :], 1.0).then_inc(cleared, 1)
            selv = PT[:, 2, 0:E * 128].rearrange("p (e m) -> p e m", e=E)
            g.memset(selv, 0.0).then_inc(cleared, 1)
            g.memset(bparts[:, :, :], 1.0).then_inc(cleared, 1)
            g.memset(ones[:, :], 1.0).then_inc(shaped, 1)
            g.iota(iota_i[:, :], [[1, E]], base=0, channel_multiplier=0).then_inc(counted, 1)
            g.iota(rest_i[:, :], [[-128, NT]], base=L - 1, channel_multiplier=-1).then_inc(counted, 1)
            pool.wait_ge(cleared, 4)
            g.affine_select(out=ident[:, :], in_=ident[:, :], compare_op=ALU.not_equal, fill=1.0, base=0,
                            pattern=[[-1, 128]], channel_multiplier=1).then_inc(shaped, 1)
            g.affine_select(out=below[:, :], in_=below[:, :], compare_op=ALU.is_gt, fill=0.0, base=0,
                            pattern=[[-1, 128]], channel_multiplier=1).then_inc(shaped, 1)
            g.affine_select(out=bparts[:, :, :], in_=bparts[:, :, :], compare_op=ALU.is_equal, fill=0.0, base=-ROW_ADD,
                            pattern=[[-1, 3], [0, H]], channel_multiplier=1).then_inc(shaped, 1)
            g.affine_select(out=selv, in_=selv, compare_op=ALU.not_equal, fill=1.0, base=0,
                            pattern=[[-1, E], [0, 128]], channel_multiplier=1).then_inc(cleared, 1)
            pool.wait_ge(cleared, 5)
            g.affine_select(out=selv, in_=selv, compare_op=ALU.not_equal, fill=1.0, base=-32,
                            pattern=[[-1, E], [0, 128]], channel_multiplier=1).then_inc(shaped, 1)
            for n in ("K2", "K1"):
                g.memset(stack[n][:, :, :], 0.0).then_inc(cleared, 1)
            pool.wait_ge(cleared, 7)
            for n in ("K2", "K1"):
                g.memset(stack[n][ROW_ADD:ROW_ADD + 32, :, :], 1.0).then_inc(kset, 1)

            def split_steps(u, name, bt, following):
                i = ("Q2", "K2", "Q1", "K1").index(name)
                s, p, c = split[i % 2], parts[i % 2], bt * SPLIT_STEPS + 2 * i
                wait_apart(pool, *read(u, name))
                g.tensor_tensor(s[:, :], s[:, :], p[:, 0, :], ALU.subtract).then_inc(pool_step, 1)
                yield
                wait_apart(pool, pool_step, c + 1)
                g.tensor_tensor(p[:, 1, :], s[:, :], ones[:, 0:1].broadcast_to([128, L]), ALU.mult).then_inc(pool_step, 1)
                yield
                wait_apart(pool, pool_step, c + 2)
                g.tensor_tensor(p[:, 2, :], s[:, :], p[:, 1, :], ALU.subtract).then_inc(parts_ready, 1)
                yield

            def mask(it, n):
                wait_apart(pool, weighed, it * WEIGHED + 2 * (n - N1) + 2)
                w, blocks = width(n), len(ATTENTION[n][2])
                v = PT[:, n % SLOTS, 0:4 * w].rearrange("p (h n) -> p h n", n=w)[:, :, 0:128 * blocks]
                pattern = [[0, 4], [1, 128]] if blocks == 1 else [[0, 4], [0, 2], [1, 128]]
                g.affine_select(out=v, in_=v, compare_op=ALU.is_ge, fill=0.0, base=0,
                                pattern=pattern, channel_multiplier=-1).then_inc(masked, 1)

            def weigh_expert(it, e):
                k, c = score_use(it, 2 * (EXPERT + e) + 1)
                pool.wait_ge(s_read[k], c + 2)
                k, c = acc_use(it, 2 * NG + 2 * e - 1)
                pool.wait_ge(o_read[k], c + 2)
                a = AB[e % DEPTH].rearrange("p (f n) -> p f n", f=NFH)
                w = CB[(e - 1) % DEPTH].unsqueeze(1).broadcast_to([128, NFH, L])
                g.tensor_tensor(a, a, w, ALU.mult).then_inc(routed, 1)

            def row(u, it, following):
                wait_apart(pool, xn_ready, it + 1)
                wait_apart(pool, down_done, it * DOWNS + DEPTH)
                g.tensor_scalar(x1[:, :, :], xn[:, :, :], 1.0, None, ALU.mult).then_inc(carried, 1)
                for n in range(N1, UNITS):
                    mask(it, n)
                    if following and n == 21:
                        steps = split_steps(u, "Q2", it + 1, True)
                    if following and n == 24:
                        steps = split_steps(u, "K2", it + 1, True)
                    if following and 21 <= n < 27:
                        next(steps)
                for e in range(1, NE):
                    if following and e < 3:
                        for _step in split_steps(u, ("Q1", "K1")[e - 1], it + 1, True):
                            pass
                    weigh_expert(it, e)

            pool.wait_ge(kset, 2)
            pool.wait_ge(setup, 1)
            for name in ("Q2", "K2", "Q1", "K1"):
                for _step in split_steps(FIRST, name, 0, False):
                    pass
            with pool.Fori(0, B - 1) as it:
                row(LOOP.row(it), it, True)
            row(LAST, B - 1, False)

        @block.scalar
        def _(act):
            a = nc.scalar
            act.dma_start(PT[:, 0:2, :].rearrange("p s n -> p (s n)")[:, 0:NE * F].rearrange("p (e n) -> p e n", e=NE), w_gu[:, :, 0, :]).then_inc(gu_in, 16)
            act.dma_start(PT[:, 2:4, :].rearrange("p s n -> p (s n)")[:, 1024:1024 + NE * F].rearrange("p (e n) -> p e n", e=NE), w_gu[:, :, 1, :]).then_inc(gu_in, 16)
            act.dma_start(wdn[:, :, :, :], w_dn).then_inc(dn_in, 16)

            def tau():
                act.wait_ge(par_in, 16)
                a.activation(pt[0][:, :], pars[:, 0, :], ACT.Abs).then_inc(tau_step, 1)
                act.wait_ge(tau_step, 1)
                a.activation(pt[1][:, :], pt[0][:, :], ACT.Exp, scale=-1.0).then_inc(tau_step, 1)
                act.wait_ge(tau_step, 3)
                a.activation(pt[3][:, :], pt[2][:, :], ACT.Ln).then_inc(tau_step, 1)
                act.wait_ge(tau_step, 5)
                a.activation(pt[7][:, 0:H], pt[6][:, 0:H], ACT.Sigmoid).then_inc(tau_step, 1)

            def evacuate(u, name, dst, **scale):
                k, _n = u(name)
                act.wait_ge(*full(u, name))
                a.activation(dst, M[k][0:dst.shape[0], 0:dst.shape[-1]], ACT.Identity, **scale).then_inc(m_read[k], 1)

            def copy_v(u, name, V):
                k, _n = u(name)
                act.wait_ge(*full(u, name))
                a.activation(V[:, :, :, 0:HD], M[k][:, :].rearrange("p (t h d) -> p t h d", t=NT, h=H),
                             ACT.Copy).then_inc(m_read[k], 1)

            def root_norms(bt):
                act.wait_ge(roots_ready, bt + 1)
                a.activation(rinv[:, 0:2, :], root[:, 0:2, :], ACT.Sqrt).then_inc(rooted1, 1)

            def projection(u, name, bt):
                i = ("Q2", "K2", "Q1", "K1").index(name)
                k, _n = u(name)
                scale = {"Q2": {"scale": HD ** -0.5}, "Q1": {"scale": qs1[:, :]}}.get(name, {})
                if i >= 2:
                    act.wait_ge(stored[("Q2", "K2")[i - 2]], bt * 16 + 16)
                elif not isinstance(bt, int) or bt > 0:
                    act.wait_ge(stored[("Q1", "K1")[i]], bt * 16)
                act.wait_ge(*full(u, name))
                a.activation(split[i % 2][:, :], M[k][:, :], ACT.Identity, **scale)
                a.activation(parts[i % 2][:, 0, :], M[k][:, :], ACT.Identity, **scale).then_inc(m_read[k], 1)

            def take(u, name, bt):
                if name == "maxT_Y":
                    evacuate(u, name, mTY[:, :])
                elif name == "maxT_X":
                    evacuate(u, name, mTX[:, :])
                elif name == "xnT":
                    evacuate(u, name, xnT[:, :])
                elif name == "hT":
                    evacuate(u, name, hT[:, :], scale=n1s[:, :])
                elif name == "h2T":
                    evacuate(u, name, h2T[:, :], scale=n2s[:, :])
                elif name in ("ctxT2", "ctxT1"):
                    evacuate(u, name, ctxT[:, :])
                elif name == "proj1":
                    evacuate(u, name, sT[:, :])
                elif name in ("V2", "V1"):
                    copy_v(u, name, V2 if name == "V2" else V1)
                elif name in ("Q2", "K2", "Q1", "K1"):
                    projection(u, name, bt)

            def acc_out(it, G):
                k, _c = acc_use(it, G)
                last = NT * G + NT - 1 if G < NG else N1 + 3 * (G - NG) + 2
                act.wait_ge(pv_done, it * UNITS + last + 1 + SLOTS)
                a.activation(OS[:, G % NG, :], O[k][:, :], ACT.Copy).then_inc(o_read[k], 1)

            def weights(it, n):
                w = width(n)
                act.wait_ge(pv_done, it * UNITS + n + 1)
                if n in (0, 2):
                    act.wait_ge(down_done, it * DOWNS + n + 1)
                for q in range(2):
                    k, c = score_use(it, 2 * n + q)
                    act.wait_ge(s_full[k], c + 1)
                    a.activation(PT[:, n % SLOTS, 2 * q * w:2 * q * w + 2 * w].rearrange("p (r n) -> p r n", r=2),
                                 S[k][:, :].rearrange("p (r n) -> p r n", r=2)[:, :, 0:w],
                                 ACT.Exp if n < N1 else ACT.Sigmoid).then_inc(s_read[k], 1)

            def routing_weights(it, e):
                k, c = acc_use(it, 2 * NG + 2 * e - 1)
                act.wait_ge(cb_full, it * E + e)
                act.wait_ge(routed, it * E + e)
                a.activation(CB[(e - 1) % DEPTH], O[k][:, :], ACT.Copy).then_inc(o_read[k], 1)

            def row(u, it, following):
                bt = it + 1
                outs = {**{NT * G + NT + 2: G for G in range(NG)}, **{N1 + 3 * g + 6: NG + g for g in range(NG - 2)},
                        UNITS - 1: 2 * NG - 2}
                for n in range(UNITS):
                    if n == N1 and following:
                        root_norms(bt)
                    weights(it, n)
                    if n == N1 + 6:
                        act.wait_ge(*full(u, ("oT2", NT - 1)))
                    if n in outs:
                        acc_out(it, outs[n])
                    for name in u.places[n]:
                        take(u, name, bt)
                    if n == 24:
                        act.wait_ge(*read(u, "proj2"))
                        for t in range(NT):
                            a.activation(h2t[:, t, :], x1[:, t, :], ACT.Square, accum_out=ssum[:, t:t + 1]).then_inc(squared, 1)
                        act.wait_ge(squared, (it + 1) * NT)
                        a.activation(rinv[:, 2, :], ssum[:, :], ACT.Sqrt, scale=1.0 / D, bias=eps6[:, :]).then_inc(rooted2, 1)
                act.wait_ge(*read(u, "logits"))
                a.activation(lp[:, :, :], ld[:, :, :], ACT.Sigmoid).then_inc(exps_ready, 1)
                a.activation(lq[:, :, :], ld[:, :, :], ACT.Sigmoid, scale=-1.0).then_inc(exps_ready, 1)
                for e in range(NE):
                    if e >= 2:
                        routing_weights(it, e - 1)
                    k, c = score_use(it, 2 * (EXPERT + e))
                    act.wait_ge(s_full[k], c + 1)
                    act.wait_ge(down_done, it * DOWNS + e + 1)
                    if e < DEPTH:
                        act.wait_ge(pv_done, it * UNITS + UNITS + e + 1)
                    a.activation(AB[e % DEPTH], S[k][:, :], ACT.Silu).then_inc(s_read[k], 1)
                    if e == 0:
                        acc_out(it, 2 * NG - 1)
                    for name in u.places[EXPERT + e]:
                        take(u, name, bt)
                    if e == 0:
                        act.wait_ge(gap_ready, it + 1)
                        a.activation(wgap[:, :], dtop[:, :], ACT.Tanh, scale=0.5).then_inc(top_ready, 1)
                    if e == NE - 1:
                        routing_weights(it, e)
                act.wait_ge(down_done, it * DOWNS + DOWNS + DEPTH)
                a.activation(gT[:, :], O[0][:, :], ACT.Silu).then_inc(o_read[0], 1)

            root_norms(0)
            tau()
            act.wait_ge(w_in, 80)
            for n in FIRST.places:
                for name in FIRST.places[n]:
                    if name == "Q2":
                        act.wait_ge(setup, 1)
                    take(FIRST, name, 0)
            with act.Fori(0, B - 1) as it:
                row(LOOP.row(it), it, True)
            row(LAST, B - 1, False)

        @block.vector
        def _(dve):
            v = nc.vector
            steps = [0, 0]

            def step(ins, apart=False):
                ins.then_inc(dve_step, 1)
                steps[0] += 1
                if apart:
                    wait_apart(dve, dve_step, steps[1] + steps[0])
                else:
                    dve.wait_ge(dve_step, steps[1] + steps[0])

            def norm_stats(bt):
                dve.wait_ge(xin_in, bt * 16 + 16)
                for t in range(NT):
                    last = v.bn_stats(stats[:, t, :], xin[:, t, :])
                step(last, apart=True)
                for t in range(NT):
                    last = v.bn_aggr(mv[:, t, :], stats[:, t, :])
                step(last)
                v.tensor_scalar(root[:, 0, :], mv[:, :, 1], 1e-5, None, ALU.add)
                v.tensor_scalar(root[:, 1, :], mv[:, :, 1], 1.0 + 1e-6, 1e-11, ALU.mult, ALU.add).then_inc(roots_ready, 1)

            def norm_apply(bt):
                dve.wait_ge(rooted1, bt + 1)
                step(v.reciprocal(rinv[:, 0:2, :], rinv[:, 0:2, :]))
                for dst, i, ready in ((xn, 0, xn_ready), (ht, 1, h_ready)):
                    for t in range(NT):
                        last = v.tensor_scalar(dst[:, t, :], xin[:, t, :], mv[:, t, 0:1], rinv[:, i, t:t + 1],
                                               ALU.subtract, ALU.mult)
                    last.then_inc(ready, 1)

            def maximum(u, name):
                _m, h, t = name
                k, _n = u(name)
                dve.wait_ge(*full(u, name))
                v.tensor_reduce(nmax[:, h, t:t + 1], M[k][:, :], AX.X, ALU.max, negate=True).then_inc(m_read[k], 1)

            def maxima_parts(u, blocks, dst, ready):
                for b in blocks[-2:]:
                    dve.wait_ge(*read(u, b))
                h0, h1 = blocks[0][1], blocks[-1][1] + 1
                src = nmax[:, h0:h1, :].rearrange("p h t -> p (h t)")
                step(v.tensor_copy(dst[:, 0, :], src))
                v.tensor_tensor(dst[:, 1, :], src, dst[:, 0, :], ALU.subtract).then_inc(ready, 1)

            def attention_out(u, name, t):
                k, _n = u((name, t))
                w = M[k][:, :].rearrange("p (g q c) -> p (g q) c", g=NG, c=32)
                dve.wait_ge(*full(u, (name, t)))
                if name == "oT1":
                    step(v.tensor_tensor(dsum[:, t, :], w[:, :, HD], dcorr[:, t, :], ALU.add))
                    v.tensor_tensor(corr[:, t, :].rearrange("p (h d) -> p h d", h=H), w[:, :, 0:HD],
                                    corr[:, t, :].rearrange("p (h d) -> p h d", h=H), ALU.add).then_inc(m_read[k], 1)
                    step(v.reciprocal(rden[:, t, :], dsum[:, t, :]))
                    dve.wait_ge(*read(u, (name, t)))
                    v.tensor_tensor(ctxs[:, t, :].rearrange("p (h d) -> p h d", h=H),
                                    corr[:, t, :].rearrange("p (h d) -> p h d", h=H),
                                    rden[:, t, :].unsqueeze(2).broadcast_to([128, H, HD]), ALU.mult).then_inc(gated, 1)
                else:
                    step(v.reciprocal(rden[:, t, :], w[:, :, HD]))
                    v.tensor_tensor(ctxs[:, t, :].rearrange("p (h d) -> p h d", h=H), w[:, :, 0:HD],
                                    rden[:, t, :].unsqueeze(2).broadcast_to([128, H, HD]), ALU.mult).then_inc(m_read[k], 1)

            def weigh(it, n, q):
                k, c = score_use(it, 2 * n + q)
                dve.wait_ge(s_read[k], c + 2)
                w = width(n)
                p = PT[:, n % SLOTS, 2 * q * w:2 * q * w + 2 * w]
                v.scalar_tensor_tensor(p, p, 1.0, p, ALU.subtract, ALU.mult).then_inc(weighed, 1)

            def router(u, it):
                dve.wait_ge(exps_ready, 2 * it + 2)
                step(v.reciprocal(lq[:, :, :], lq[:, :, :]))
                step(v.tensor_tensor(lp[:, :, :], lp[:, :, :], lq[:, :, :], ALU.mult))
                step(v.tensor_reduce(lsum[:, :], lp[:, :, :], AX.X, ALU.add))
                step(v.reciprocal(lsum[:, :], lsum[:, :]))
                step(v.tensor_tensor(lp[:, :, :], lp[:, :, :], lsum[:, :].unsqueeze(2).broadcast_to([128, NT, E]), ALU.mult), apart=True)
                for t in range(NT):
                    last = v.max(top[:, t, :], lp[:, t, :])
                step(last)
                v.tensor_tensor(dtop[:, :], top[:, :, 0], top[:, :, 1], ALU.subtract).then_inc(gap_ready, 1)
                for t in range(NT):
                    last = v.max_index(topi[:, t, :], top[:, t, :], lp[:, t, :])
                step(last)
                step(v.tensor_copy(topf[:, :, :], topi[:, :, :]))

            def combine(it):
                dve.wait_ge(top_ready, it + 1)
                for i, half in ((0, 0.5), (1, -0.5)):
                    last = v.tensor_scalar(wtop[:, i, :], wgap[:, :], half, 0.5, ALU.mult, ALU.add)
                step(last)
                shape = [128, NT, E]
                for i, dst in ((0, lp), (1, lq)):
                    step(v.tensor_tensor(dst[:, :, :], iota_f[:, :].unsqueeze(1).broadcast_to(shape),
                                         topf[:, :, i:i + 1].broadcast_to(shape), ALU.is_equal))
                    step(v.tensor_tensor(dst[:, :, :], dst[:, :, :], wtop[:, i, :].unsqueeze(2).broadcast_to(shape), ALU.mult))
                v.tensor_tensor(comb[:, :, :], lp[:, :, :], lq[:, :, :], ALU.add).then_inc(comb_ready, 1)

            def take(u, it, name):
                k, _n = u(name)
                if name[0] == "max":
                    maximum(u, name)
                elif name[0] in ("oT1", "oT2"):
                    if name == ("oT1", 0):
                        dve.wait_ge(*read(u, "suffix"))
                    attention_out(u, *name)
                elif name == "proj2":
                    dve.wait_ge(*full(u, name))
                    dve.wait_ge(carried, it + 1)
                    v.tensor_tensor(x1[:, :, :].rearrange("p t d -> p (t d)"), M[k][:, :],
                                    x1[:, :, :].rearrange("p t d -> p (t d)"), ALU.add).then_inc(m_read[k], 1)
                elif name == "logits":
                    dve.wait_ge(*full(u, name))
                    lg = M[k][:, 0:NT * E].rearrange("p (t e) -> p t e", t=NT)
                    step(v.tensor_reduce(lmax[:, :], lg, AX.X, ALU.max))
                    v.tensor_tensor(ld[:, :, :], lg, lmax[:, :].unsqueeze(2).broadcast_to([128, NT, E]),
                                    ALU.subtract).then_inc(m_read[k], 1)
                    router(u, it)
                elif name == "suffix":
                    dve.wait_ge(*full(u, name))
                    v.tensor_tensor(corr[:, :, :].rearrange("p t (h d) -> p t h d", h=H),
                                    M[k][:, :].rearrange("p (t h d) -> p t h d", t=NT, h=H),
                                    cneg[:, :].unsqueeze(1).unsqueeze(3).broadcast_to([128, NT, H, HD]),
                                    ALU.mult).then_inc(m_read[k], 1)
                elif name == "combT":
                    dve.wait_ge(*full(u, name))
                    step(v.tensor_copy(cT[0:E, :], M[k][0:E, :]))
                    v.tensor_tensor(cT[32:32 + E, :], M[k][0:E, :], cT[0:E, :], ALU.subtract).then_inc(m_read[k], 1)

            def row(u, it, following):
                bt = it + 1
                steps[0] = 0
                for n in range(N1):
                    for name in u.places[n]:
                        take(u, it, name)
                    if n == 7:
                        maxima_parts(u, MAX_Y, mhY, maxY_ready)
                        if following:
                            norm_stats(bt)
                if following:
                    dve.wait_ge(carried, it + 1)
                    norm_apply(bt)
                for n in range(N1, UNITS):
                    for q in range(2):
                        weigh(it, n, q)
                    for name in u.places[n]:
                        take(u, it, name)
                    if n == 25:
                        dve.wait_ge(rooted2, it + 1)
                        step(v.reciprocal(rinv[:, 2, :], rinv[:, 2, :]))
                        for t in range(NT):
                            last = v.tensor_scalar(h2t[:, t, :], x1[:, t, :], rinv[:, 2, t:t + 1], None, ALU.mult)
                        last.then_inc(h2_ready, 1)
                dve.wait_ge(*read(u, "h2T"))
                step(v.tensor_copy(h2hi[:, :], h2T[:, :]))
                v.tensor_tensor(h2lo[:, :], h2T[:, :], h2hi[:, :], ALU.subtract).then_inc(h2r_ready, 1)
                for e in range(NE):
                    work = u.places[EXPERT + e]
                    early = len(work) if e == 0 else 4
                    if e == 0:
                        take(u, it, "logits")
                    else:
                        for name in work[:early]:
                            take(u, it, name)
                    k, c = score_use(it, 2 * (EXPERT + e))
                    k2, c2 = score_use(it, 2 * (EXPERT + e) + 1)
                    dve.wait_ge(s_read[k], c + 2)
                    dve.wait_ge(s_full[k2], c2 + 1)
                    v.tensor_tensor(AB[e % DEPTH], AB[e % DEPTH], S[k2][:, :], ALU.mult).then_inc(s_read[k2], 1)
                    if e == 0:
                        take(u, it, "suffix")
                        combine(it)
                    for name in work[early:]:
                        take(u, it, name)
                if following:
                    maxima_parts(u, MAX_X, mhX, maxX_ready)
                dve.wait_ge(o_read[0], it * O_USES[0] + O_USES[0] + 1)
                dve.wait_ge(*read(u, "proj1"))
                v.tensor_tensor(gT[:, :], gT[:, :], sT[:, :], ALU.mult).then_inc(prod_ready, 1)
                k, _n = u("outT")
                dve.wait_ge(*full(u, "outT"))
                dve.wait_ge(xres_in, it * 16 + 16)
                v.tensor_tensor(xres[:, :, :].rearrange("p t d -> p (t d)"), M[k][:, :],
                                xres[:, :, :].rearrange("p t d -> p (t d)"), ALU.add).then_inc(m_read[k], 1)
                assert steps[0] <= DVE_ROW and (not following or steps[0] == DVE_ROW), steps

            for k in range(2):
                v.memset(M[k][:, :], 0.0).then_inc(m_read[k], 1)
            norm_stats(0)
            norm_apply(0)
            for k in range(2):
                v.memset(S[k][:, :], 0.0).then_inc(s_read[k], 1)
                v.memset(O[k][:, :], 0.0).then_inc(o_read[k], 1)
            v.memset(eps6[:, :], 1e-6)
            v.memset(stack["Q2"][:, :, :].bitcast(dt.uint32), 0)
            v.memset(stack["Q1"][:, :, :].bitcast(dt.uint32), 0)
            v.memset(V1[:, :, :, :], 0.0)
            v.memset(V2[:, :, :, :], 0.0)
            step(v.memset(cT[:, :].bitcast(fp32), 0.0))
            v.memset(V1[:, :, :, HD:HD + 1], 1.0)
            v.memset(V2[:, :, :, HD:HD + 1], 1.0)
            dve.wait_ge(tau_step, 2)
            v.tensor_scalar(pt[2][:, :], pt[1][:, :], 1.0, None, ALU.add).then_inc(tau_step, 1)
            dve.wait_ge(tau_step, 4)
            step(v.tensor_scalar(pt[4][:, :], pt[2][:, :], -1.0, None, ALU.add))
            step(v.tensor_scalar(pt[5][:, :], pt[4][:, :], 0.0, None, ALU.is_equal))
            step(v.tensor_tensor(pt[6][:, :], pt[4][:, :], pt[5][:, :], ALU.add))
            step(v.reciprocal(pt[6][:, :], pt[6][:, :]))
            step(v.tensor_tensor(pt[6][:, :], pt[6][:, :], pt[3][:, :], ALU.mult))
            step(v.tensor_tensor(pt[6][:, :], pt[6][:, :], pt[5][:, :], ALU.add))
            step(v.tensor_tensor(pt[6][:, :], pt[6][:, :], pt[1][:, :], ALU.mult))
            step(v.scalar_tensor_tensor(pt[6][:, :], pars[:, 0, :], 0.0, pt[6][:, :], ALU.max, ALU.add))
            step(v.tensor_scalar(pt[6][:, :], pt[6][:, :], 1e-6, None, ALU.add))
            step(v.reciprocal(pt[5][:, :], pt[6][:, :]))
            step(v.tensor_scalar(pt[3][:, :], pt[5][:, :], 2.0, None, ALU.mult))
            v.tensor_scalar(qs1[:, :], pt[3][:, H:H + 1], HD ** -0.5, None, ALU.mult)
            step(v.scalar_tensor_tensor(pt[4][:, :], pars[:, 1, :], -1.0, pt[3][:, :], ALU.mult, ALU.mult))
            v.scalar_tensor_tensor(pt[6][:, :], pt[3][:, :], MASKED, pt[4][:, :], ALU.mult, ALU.add).then_inc(tau_step, 1)
            step(v.tensor_copy(bsplit[:, 0, :], pt[4][:, 0:H]))
            step(v.tensor_tensor(pt[5][:, 0:H], pt[4][:, 0:H], bsplit[:, 0, :], ALU.subtract))
            step(v.tensor_copy(bsplit[:, 1, :], pt[5][:, 0:H]))
            step(v.tensor_tensor(bsplit[:, 2, :], pt[5][:, 0:H], bsplit[:, 1, :], ALU.subtract))
            dve.wait_ge(shaped, 5)
            step(v.tensor_tensor(bparts[:, :, :], bparts[:, :, :], bsplit[:, :, :], ALU.mult))
            step(v.tensor_reduce(brow[:, :], bparts[:, :, :].rearrange("p a h -> p h a"), AX.X, ALU.add))
            step(v.tensor_copy(stack["Q1"][ROW_ADD:ROW_ADD + 32, :, :],
                               brow[ROW_ADD:ROW_ADD + 32, :].unsqueeze(2).broadcast_to([32, H, L])))
            dve.wait_ge(counted, 2)
            v.tensor_copy(iota_f[:, :], iota_i[:, :])
            step(v.tensor_copy(rest_f[:, :], rest_i[:, :]))
            dve.wait_ge(tau_step, 6)
            step(v.scalar_tensor_tensor(cneg[:, :], pt[7][:, 0:H], 1.0, pt[7][:, 0:H], ALU.subtract, ALU.mult))
            step(v.tensor_tensor(dcorr[:, :, :], rest_f[:, :].unsqueeze(2).broadcast_to([128, NT, H]),
                                 cneg[:, :].unsqueeze(1).broadcast_to([128, NT, H]), ALU.mult))
            step(v.tensor_scalar(dcorr[:, :, :], dcorr[:, :, :], -2.5e-7, None, ALU.add))
            step(v.tensor_copy(identb[:, :], ident[:, :]))
            v.tensor_copy(sel[:, :, :], PT[:, 2, 0:E * 128].rearrange("p (e m) -> p e m", e=E)).then_inc(setup, 1)
            dve.wait_ge(gu_in, 32)
            for i, src in enumerate((PT[:, 0:2, :].rearrange("p s n -> p (s n)")[:, 0:NE * F],
                                     PT[:, 2:4, :].rearrange("p s n -> p (s n)")[:, 1024:1024 + NE * F])):
                src = src.rearrange("p (e n) -> p e n", e=NE)
                step(v.tensor_copy(wgu_hi[:, :, i * F:i * F + F], src))
                last = v.tensor_tensor(wgu_lo[:, :, i * F:i * F + F], src, wgu_hi[:, :, i * F:i * F + F], ALU.subtract)
            last.then_inc(pv_done, SLOTS)
            dve.sem_inc(routed, DEPTH)
            dve.sem_inc(down_done, DEPTH)
            for name in MAX_X:
                maximum(FIRST, name)
            maxima_parts(FIRST, MAX_X, mhX, maxX_ready)
            assert steps[0] == DVE_FIRST
            steps[1] = DVE_FIRST
            with dve.Fori(0, B - 1) as it:
                steps[1] = DVE_FIRST + it * DVE_ROW
                row(LOOP.row(it), it, True)
            steps[1] = DVE_FIRST + (B - 1) * DVE_ROW
            row(LAST, B - 1, False)

        @block.tensor
        def _(pe):
            t_ = nc.tensor
            order, uses = [], [None]

            def begin(u, name):
                order.append(name)
                assert u.order[len(order) - 1] == name, (name, u.order[len(order) - 1])
                k, _n = u(name)
                pe.wait_ge(*free(u, name))
                return k

            def transposed(u, name, src):
                k = begin(u, name)
                for t in range(NT):
                    last = t_.transpose(M[k][:, t * 128:t * 128 + 128], src[:, t, :], ident[:, :])
                last.then_inc(m_full[k], 1)

            def projected(u, name, w, src):
                k = begin(u, name)
                t_.matmul(M[k][:, :], w, src[:, :], start=True, stop=True).then_inc(m_full[k], 1)

            def projected_v(u, name, w, src):
                k = begin(u, name)
                for t in range(NT):
                    last = t_.matmul(M[k][:, t * 128:t * 128 + 128], src[:, t * 128:t * 128 + 128], w, start=True, stop=True)
                last.then_inc(m_full[k], 1)

            def maximum(u, name):
                k = begin(u, name)
                _m, h, t = name
                t_.matmul(M[k][:, :], stack["Q2"][0:ROW_ADD, h, t * 128:t * 128 + 128], stack["K2"][0:ROW_ADD, h, :],
                          start=True, stop=True).then_inc(m_full[k], 1)

            def maxima_T(u, name, src, ready, n):
                pe.wait_ge(ready, n + 1)
                k = begin(u, name)
                t_.matmul(M[k][0:src.shape[1] * src.shape[2], 0:128], src[:, :, :], identb[:, :], start=True, stop=True)\
                    .then_inc(m_full[k], 1)

            def out_T(u, name, t):
                k = begin(u, (name, t))
                for hg in range(NG):
                    last = t_.transpose(M[k][:, hg * 128:hg * 128 + 128], OS[:, hg, t * 128:t * 128 + 128], ident[:, :])
                last.then_inc(m_full[k], 1)

            def scores(it, n, q):
                k, c = score_use(it, 2 * n + q)
                pe.wait_ge(s_read[k], c + 1)
                g, _kind, js = ATTENTION[n]
                key, query = ("K2", "Q2") if n < N1 else ("K1", "Q1")
                for r in range(2):
                    h, at = 4 * g + 2 * q + r, 512 * r
                    for j in js:
                        i0 = 0 if n < N1 else 128 * j
                        last = t_.matmul(S[k][:, at:at + L - i0], stack[key][:, h, 128 * j:128 * j + 128],
                                         stack[query][:, h, i0:L], start=True, stop=True)
                        at += L - i0
                last.then_inc(s_full[k], 1)

            def with_v(it, n):
                g, _kind, js = ATTENTION[n]
                G, V, w = (g, V2, width(n)) if n < N1 else (NG + g, V1, width(n))
                k, c = acc_use(it, G)
                if js[0] == 0:
                    pe.wait_ge(o_read[k], c + 1)
                if n < N1:
                    for i in range(2):
                        pe.wait_ge(s_read[i], it * S_USES + n + 2)
                else:
                    pe.wait_ge(masked, it * len(STAGE2) + n - N1 + 1)
                at = 0
                for j in js:
                    i0 = 0 if n < N1 else 128 * j
                    for q in range(4):
                        last = t_.matmul(O[k][32 * q:32 * q + VW, i0:L], V[:, j, 4 * g + q, :],
                                         PT[:, n % SLOTS, w * q + at:w * q + at + L - i0],
                                         start=(j == 0), stop=(NT - 1 in js and j == js[-1]))
                    at += L - i0
                last.then_inc(pv_done, 1)

            def routing_weights(it, e):
                k, c = acc_use(it, 2 * NG + 2 * e - 1)
                pe.wait_ge(o_read[k], c + 1)
                t_.matmul(O[k][:, :], sel[:, e - 1, :], cT[:, :], start=True, stop=True).then_inc(cb_full, 1)

            def second_product(it, e):
                if e == 0:
                    pe.wait_ge(o_read[0], it * O_USES[0] + NG + 1)
                    k, c = score_use(it, 2 * EXPERT + 1)
                    pe.wait_ge(s_read[k], c + 2)
                else:
                    pe.wait_ge(routed, it * E + e + DEPTH)
                for f in range(NFH):
                    last = t_.matmul(O[0][:, :], wdn[:, e, f, :], AB[e % DEPTH][:, f * 512:f * 512 + 512],
                                     start=(e == 0 and f == 0), stop=(e == NE - 1 and f == NFH - 1))
                    if f == 0:
                        yield
                last.then_inc(down_done, 1)
                yield

            def expert(it, e):
                if e == 2:
                    pe.wait_ge(*read(uses[0], "combT"))
                if e >= 2:
                    routing_weights(it, e - 1)
                for i in range(2):
                    k, c = score_use(it, 2 * (EXPERT + e) + i)
                    pe.wait_ge(s_read[k], c + 1)
                    for f in range(NFH):
                        cols = slice(i * F + f * 128, i * F + f * 128 + 128)
                        dst = S[k][:, f * 512:f * 512 + 512]
                        t_.matmul(dst, wgu_hi[:, e, cols], h2hi[:, :], start=True, stop=False)
                        t_.matmul(dst, wgu_hi[:, e, cols], h2lo[:, :], start=False, stop=False)
                        last = t_.matmul(dst, wgu_lo[:, e, cols], h2hi[:, :], start=False, stop=True)
                        if f == NFH - 1:
                            last.then_inc(s_full[k], 1)
                        yield
                if e >= 2:
                    yield from second_product(it, e - 2)

            def work(u, it, name):
                bt = it + 1
                if name[0] == "max":
                    if name == MAX_X[0]:
                        for n in ("Q2", "K2"):
                            pe.wait_ge(stacked[n], (bt + 1) * 16 * len(PAIRS))
                    maximum(u, name)
                elif name == "maxT_Y":
                    maxima_T(u, name, mhY, maxY_ready, it)
                elif name == "maxT_X":
                    maxima_T(u, name, mhX, maxX_ready, bt)
                elif name == "xnT":
                    pe.wait_ge(xn_ready, bt + 1)
                    transposed(u, name, xn)
                elif name == "hT":
                    pe.wait_ge(h_ready, bt + 1)
                    transposed(u, name, ht)
                elif name in ("Q2", "K2", "Q1", "K1"):
                    if name == "Q2":
                        pe.wait_ge(*read(u, "xnT"))
                        pe.wait_ge(*read(u, "hT"))
                    w, src = (w2s, hT) if name[1] == "2" else (w1s, xnT)
                    projected(u, name, w[:, 0 if name[0] == "Q" else 1, :], src)
                elif name in ("V2", "V1"):
                    projected_v(u, name, (w2s if name == "V2" else w1s)[:, 2, :], hT if name == "V2" else xnT)
                elif name[0] in ("oT2", "oT1"):
                    if name[1] == 0:
                        done = NG // 2 if name[0] == "oT2" else NG
                        pe.wait_ge(o_read[0], it * O_USES[0] + done + 1)
                        pe.wait_ge(o_read[1], it * O_USES[1] + done + 1)
                    out_T(u, *name)
                elif name == "ctxT2":
                    for t in range(NT):
                        pe.wait_ge(*read(u, ("oT2", t)))
                    transposed(u, name, ctxs)
                elif name == "ctxT1":
                    pe.wait_ge(gated, (it + 1) * NT)
                    transposed(u, name, ctxs)
                elif name in ("proj2", "proj1"):
                    pe.wait_ge(*read(u, "ctxT" + name[4]))
                    if name == "proj2":
                        projected_v(u, name, w2s[:, 3, :], ctxT)
                    else:
                        projected(u, name, w1s[:, 3, :], ctxT)
                elif name == "h2T":
                    pe.wait_ge(h2_ready, it + 1)
                    transposed(u, name, h2t)
                elif name == "logits":
                    pe.wait_ge(*read(u, "h2T"))
                    k = begin(u, name)
                    for t in range(NT):
                        last = t_.matmul(M[k][:, t * E:t * E + E], h2T[:, t * 128:t * 128 + 128], rts[:, :], start=True, stop=True)
                    last.then_inc(m_full[k], 1)
                elif name == "suffix":
                    k = begin(u, name)
                    for t in range(NT):
                        for j in range(t, NT):
                            last = t_.matmul(M[k][:, t * 128:t * 128 + 128], (below if j == t else ones)[:, :],
                                             V1[:, j, :, 0:HD], start=(j == t), stop=(j == NT - 1))
                    last.then_inc(m_full[k], 1)
                elif name == "combT":
                    pe.wait_ge(comb_ready, it + 1)
                    k = begin(u, name)
                    for t in range(NT):
                        last = t_.matmul(M[k][0:E, t * 128:t * 128 + 128], comb[:, t, :], ident[:, :], start=True, stop=True)
                    last.then_inc(m_full[k], 1)
                elif name == "outT":
                    pe.wait_ge(prod_ready, it + 1)
                    k = begin(u, name)
                    for t in range(NT):
                        last = t_.transpose(M[k][:, t * 128:t * 128 + 128], gT[:, t * 128:t * 128 + 128], ident[:, :])
                    last.then_inc(m_full[k], 1)

            def row(u, it, following):
                order.clear()
                uses[0] = u
                v_at = {n: n - 2 for n in range(2, N1 + 2)} | {n: n - 3 for n in range(N1 + 3, UNITS)}
                pe.wait_ge(rowX, (it + 1) * 32)
                for n in range(UNITS):
                    if n == NT * (HX // 4):
                        pe.wait_ge(rowY, (it + 1) * 32)
                    if n == N1:
                        for name in ("Q1", "K1"):
                            pe.wait_ge(stacked[name], (it + 1) * 16 * len(PAIRS))
                    names = u.places[n]
                    scores(it, n, 0)
                    for name in names[:len(names) // 2]:
                        work(u, it, name)
                    if n in v_at:
                        with_v(it, v_at[n])
                    scores(it, n, 1)
                    for name in names[len(names) // 2:]:
                        work(u, it, name)
                with_v(it, UNITS - 3)
                work(u, it, "logits")
                pe.wait_ge(h2r_ready, it + 1)
                for e in range(NE):
                    names = [name for name in u.places[EXPERT + e] if name != "logits"]
                    steps = 6 if e >= 2 else 4
                    for i, _step in enumerate(expert(it, e)):
                        if e == 0 and i < 2:
                            with_v(it, UNITS - 2 + i)
                        for name in names[len(names) * i // steps:len(names) * (i + 1) // steps]:
                            work(u, it, name)
                routing_weights(it, NE - 1)
                for _step in second_product(it, NE - 2):
                    pass
                for t in range(NT):
                    last = t_.matmul(O[0][:, t * 128:t * 128 + 128], x1[:, t, :], ident[:, :], start=False, stop=False)
                last.then_inc(down_done, 1)
                for _step in second_product(it, NE - 1):
                    pass
                work(u, it, "outT")
                assert order == u.order

            pe.wait_ge(shaped, 5)
            pe.wait_ge(w_in, 80)
            for n in FIRST.places:
                for name in FIRST.places[n]:
                    work(FIRST, -1, name)
            pe.wait_ge(dn_in, 16)
            with pe.Fori(0, B - 1) as it:
                row(LOOP.row(it), it, True)
            row(LAST, B - 1, False)


_INS = ["x", "par", "n1w", "n2w", "w1", "w2", "router", "w_gu", "w_dn"]


def kernel(L0_attn_x, L0_attn_Wq, L0_attn_Wk, L0_attn_Wv, L0_attn_Wo, L0_attn_compressibility, L0_attn_phase_threshold,
           L0_ffn_norm1_w, L0_ffn_norm2_w, L0_ffn_wq, L0_ffn_wk, L0_ffn_wv, L0_ffn_wo, L0_ffn_router_w,
           L0_ffn_sh_gate, L0_ffn_sh_up, L0_ffn_sh_down, L0_ffn_e_gate, L0_ffn_e_up, L0_ffn_e_down):
    import numpy as np
    import concourse.bacc as bacc
    from concourse import mybir as mb
    from concourse.bass_utils import run_bass_kernel_spmd

    def per_head(v):
        v = np.asarray(v).reshape(H)
        return np.concatenate([np.broadcast_to(v, (128, H)), np.repeat(v, HD)[:, None]], axis=1)

    gate = np.concatenate([np.asarray(L0_ffn_sh_gate)[None], np.asarray(L0_ffn_e_gate)])
    up = np.concatenate([np.asarray(L0_ffn_sh_up)[None], np.asarray(L0_ffn_e_up)])
    down = np.concatenate([np.asarray(L0_ffn_sh_down)[None], np.asarray(L0_ffn_e_down)])
    arrays = {
        "x": np.asarray(L0_attn_x),
        "par": np.stack([per_head(L0_attn_compressibility), per_head(L0_attn_phase_threshold)], axis=1),
        "n1w": np.asarray(L0_ffn_norm1_w)[:, None],
        "n2w": np.asarray(L0_ffn_norm2_w)[:, None],
        "w1": np.stack([np.asarray(w).T for w in (L0_attn_Wq, L0_attn_Wk, L0_attn_Wv, L0_attn_Wo)], axis=1),
        "w2": np.stack([np.asarray(w) for w in (L0_ffn_wq, L0_ffn_wk, L0_ffn_wv, L0_ffn_wo)], axis=1),
        "router": np.asarray(L0_ffn_router_w),
        "w_gu": np.stack([gate, up], axis=1).transpose(2, 0, 1, 3),
        "w_dn": down.reshape(NE, NFH, 128, D).transpose(2, 0, 1, 3),
    }
    arrays = {n: np.ascontiguousarray(a) for n, a in arrays.items()}
    nc = bacc.Bacc("TRN2", target_bir_lowering=False, num_devices=1)
    args = [nc.dram_tensor("in_" + n, arrays[n].shape, mb.dt.from_np(arrays[n].dtype), kind="ExternalInput").ap() for n in _INS]
    out = nc.dram_tensor("out_0", (B, L, D), mb.dt.float32, kind="ExternalOutput").ap()
    program(nc, *args, out)
    r = run_bass_kernel_spmd(nc, [{"in_" + n: arrays[n] for n in _INS}], core_ids=[0])
    return r.results[0]["out_0"]
```

```python
import concourse.bass as bass
from concourse import mybir
from contextlib import ExitStack

B, L, D = 8, 512, 128
H, HD = 16, 8
E, F = 8, 256
NE = E + 1
NT = L // 128
NG = H // 4
VW = 12
NFH = F // 128
PAIRS = [(0, 0), (0, 1), (0, 2), (1, 0), (1, 1), (2, 0)]
ROW_ADD = 64
RUNS = {"X": (0, 8), "Y": (8, 12), "Z": (12, 16)}
MASKED = -10000.0

STAGE1 = [(g, "all", [j]) for g in range(NG) for j in range(NT)]
STAGE2 = [(g, kind, js) for g in range(NG) for kind, js in (("first", [0]), ("second", [1]), ("rest", [3, 2]))]
ATTENTION = STAGE1 + STAGE2
N1, UNITS = len(STAGE1), len(ATTENTION)
SLOTS = 4


def width(n):
    _g, kind, js = ATTENTION[n]
    return L if kind == "all" else sum(L - 128 * j for j in js)


MAX = {run: [("max", h, t) for h in range(*heads) for t in range(NT)] for run, heads in RUNS.items()}
EXPERT, END = UNITS, UNITS + NE
PLACES = {n: [] for n in range(END + 1)}


def spread(work, counts):
    at = 0
    for n, count in counts.items():
        PLACES[n] += work[at:at + count]
        at += count
    assert at == len(work)


spread(MAX["Y"], {0: 1, 1: 4, 2: 4, 3: 4, 4: 3})
spread(MAX["Z"], {4: 1, 5: 3, 6: 4, 7: 4, 8: 4})
PLACES[5].insert(2, "maxT_Y")
PLACES[9] += ["maxT_Z"]
PLACES[16] += ["xnT", "hT"]
PLACES[17] += ["Q2"]
PLACES[18] += ["K2"]
PLACES[19] += ["V2", ("oT2", 0)]
PLACES[20] += [("oT2", 1), ("oT2", 2)]
PLACES[21] += [("oT2", 3)]
PLACES[22] += ["ctxT2"]
PLACES[23] += ["proj2"]
PLACES[25] += ["Q1"]
PLACES[26] += ["h2T"]
PLACES[27] += ["logits", "K1"]
PLACES[EXPERT] += ["suffix"]
PLACES[EXPERT + 1] += [("oT1", 0), "combT", ("oT1", 1)]
PLACES[EXPERT + 3] += [("oT1", 2), ("oT1", 3)]
spread(MAX["X"], {EXPERT + e: n for e, n in enumerate((0, 0, 5, 4, 4, 5, 6, 6, 2))})
PLACES[EXPERT + 4].insert(2, "V1")
PLACES[EXPERT + 4].insert(4, "ctxT1")
PLACES[EXPERT + 5].insert(2, "proj1")
PLACES[END - 1] += ["maxT_X"]
PLACES[END] += ["outT"]
AHEAD = {"xnT", "hT", "Q2", "K2", "V2", "Q1", "K1", "V1", "maxT_X", *MAX["X"]}


class Uses:

    def __init__(self, own, following, before=(0, 0)):
        self.places = {n: [w for w in work if (following if w in AHEAD else own)] for n, work in PLACES.items()}
        self.order = [w for n in sorted(self.places) for w in self.places[n]]
        self.at = {name: n for n, name in enumerate(self.order)}
        self.total = [(len(self.order) + 1) // 2, len(self.order) // 2]
        self.before = before

    def __call__(self, name):
        n = self.at[name]
        return n % 2, self.before[n % 2] + n // 2

    def row(self, it):
        later = Uses.__new__(Uses)
        later.places, later.order, later.at, later.total = self.places, self.order, self.at, self.total
        later.before = tuple(b + it * t for b, t in zip(self.before, self.total))
        return later


FIRST = Uses(False, True)
LOOP = Uses(True, True, FIRST.total)
LAST = Uses(True, False, LOOP.row(B - 1).before)

S_USES = UNITS + NE
O_USES = (2 * NG // 2 + 1, 2 * NG // 2 + E)
WEIGHED = 2 * len(STAGE2)
DOWNS = NE + 1
DEPTH = 3
DVE_FIRST, DVE_ROW = 39, 56
SPLIT_STEPS = 8


def program(nc, x, par, n1w, n2w, w1, w2, router, w_gu, w_dn, out):
    dt, ALU, ACT, AX = mybir.dt, mybir.AluOpType, mybir.ActivationFunctionType, mybir.AxisListType
    fp32, fp32r, bf16 = dt.float32, dt.float32r, dt.bfloat16

    ctx_ = ExitStack()
    with ctx_:
        def sb(name, shape, t=fp32):
            return ctx_.enter_context(nc.sbuf_tensor(name, shape, t))

        def sem(name):
            return ctx_.enter_context(nc.semaphore(name))

        xin = sb("xin", [128, NT, D])
        xres = sb("xres", [128, NT, D])
        xn = sb("xn", [128, NT, D])
        ht = sb("ht", [128, NT, D])
        x1 = sb("x1", [128, NT, D])
        h2t = sb("h2t", [128, NT, D])
        ctxs = ht
        ctxT = sb("ctxT", [128, L])
        xnT = sb("xnT", [128, L])
        hT = sb("hT", [128, L])
        h2T = sb("h2T", [128, L])
        h2hi = sb("h2hi", [128, L], fp32r)
        h2lo = sb("h2lo", [128, L], fp32r)
        sT = sb("sT", [128, L])
        gT = h2T
        corr = h2T[:, :].rearrange("p (t d) -> p t d", t=NT)
        split = [sb(f"split{i}", [128, L]) for i in range(2)]
        parts = [sb(f"parts{i}", [128, 3, L], bf16) for i in range(2)]
        stack = {n: sb("stack" + n, [128, H, L], bf16) for n in ("Q2", "K2", "Q1", "K1")}
        V2 = sb("V2", [128, NT, H, VW])
        V1 = sb("V1", [128, NT, H, VW])
        PT = sb("PT", [128, SLOTS, 4 * L])
        AB = [PT[:, i, 0:NFH * L] for i in range(DEPTH)]
        CB = [PT[:, i, NFH * L:NFH * L + L] for i in range(DEPTH)]
        OS = sb("OS", [128, NG, L])
        cT = sb("cT", [128, L], fp32r)
        wgu_hi = sb("wgu_hi", [128, NE, 2 * F], fp32r)
        wgu_lo = sb("wgu_lo", [128, NE, 2 * F], fp32r)
        wdn = sb("wdn", [128, NE, NFH, D])
        w1s = sb("w1s", [128, 4, D])
        w2s = sb("w2s", [128, 4, D])
        rts = sb("rts", [128, E])
        n1s = sb("n1s", [128, 1])
        n2s = sb("n2s", [128, 1])
        ident = sb("ident", [128, 128])
        identb = sb("identb", [128, 128], bf16)
        below = sb("below", [128, 128])
        ones = sb("ones", [128, 128])
        sel = sb("sel", [128, E, 128], fp32r)
        nmax = sb("nmax", [128, H, NT])
        count = {run: (h1 - h0) * NT for run, (h0, h1) in RUNS.items()}
        mh = {run: sb("mh" + run, [128, 2, n], bf16) for run, n in count.items()}
        mT = {run: sb("mT" + run, [2 * n, 128], bf16) for run, n in count.items()}
        stats = sb("stats", [128, NT, 6])
        mv = sb("mv", [128, NT, 2])
        root = sb("root", [128, 3, NT])
        rinv = sb("rinv", [128, 3, NT])
        newton = sb("newton", [128, 2, NT])
        ssum = sb("ssum", [128, NT])
        rden = sb("rden", [128, NT, H])
        dsum = sb("dsum", [128, NT, H])
        dcorr = sb("dcorr", [128, NT, H])
        cneg = sb("cneg", [128, H])
        qs1 = sb("qs1", [128, 1])
        pars = sb("pars", [128, 2, H + 1])
        pt = [sb(f"pt{i}", [128, H + 1]) for i in range(8)]
        bparts = sb("bparts", [128, 3, H])
        bsplit = sb("bsplit", [128, 3, H], bf16)
        brow = sb("brow", [128, H])
        iota_i = sb("iota_i", [128, E], dt.int32)
        rest_i = sb("rest_i", [128, NT], dt.int32)
        iota_f = sb("iota_f", [128, E])
        rest_f = sb("rest_f", [128, NT])
        lmax = sb("lmax", [128, NT])
        ld = sb("ld", [128, NT, E])
        lp = sb("lp", [128, NT, E])
        lq = sb("lq", [128, NT, E])
        lsum = sb("lsum", [128, NT])
        wgap = sb("wgap", [128, NT])
        top = sb("top", [128, NT, 8])
        topi = sb("topi", [128, NT, 8], dt.uint32)
        topf = sb("topf", [128, NT, 8])
        dtop = sb("dtop", [128, NT])
        wtop = sb("wtop", [128, 2, NT])
        comb = sb("comb", [128, NT, E])
        gu_raw = [PT[:, 2 * i:2 * i + 2, :].rearrange("p s n -> p (s n)")[:, 4096 - NE * F:4096]
                  .rearrange("p (e n) -> p e n", e=NE) for i in range(2)]
        scratch = {n: nc.dram_tensor("scr" + n, [3, 128, L], bf16).ap() for n in stack}

        def pb(name, cols):
            return ctx_.enter_context(nc.psum_tensor(name, [128, cols], fp32))

        S = [pb("S0", 1024), pb("S1", 1024)]
        O = [pb("O0", 512), pb("O1", 512)]
        M = [pb("M0", 512), pb("M1", 512)]

        s_full, s_read = [sem("s_full0"), sem("s_full1")], [sem("s_read0"), sem("s_read1")]
        m_full, m_read = [sem("m_full0"), sem("m_full1")], [sem("m_read0"), sem("m_read1")]
        o_read = [sem("o_read0"), sem("o_read1")]
        pv_done = sem("pv_done")
        weighed = sem("weighed")
        masked = sem("masked")
        cb_full = sem("cb_full")
        routed = sem("routed")
        routed_last = sem("routed_last")
        down_done = sem("down_done")
        xn_ready, h_ready, h2_ready, h2r_ready = (sem(n) for n in ("xn_ready", "h_ready", "h2_ready", "h2r_ready"))
        squared = sem("squared")
        exps_ready, gap_ready, top_ready, comb_ready = (sem(n) for n in ("exps_ready", "gap_ready", "top_ready", "comb_ready"))
        parts_ready, prod_ready = sem("parts_ready"), sem("prod_ready")
        max_ready = {run: sem("max_ready" + run) for run in RUNS}
        stored = {n: sem("stored" + n) for n in stack}
        stacked = {n: sem("stacked" + n) for n in stack}
        row_in = {run: sem("row_in" + run) for run in RUNS}
        xin_in, xres_in, written = sem("xin_in"), sem("xres_in"), sem("written")
        par_in, w_in, gu_in, dn_in = sem("par_in"), sem("w_in"), sem("gu_in"), sem("dn_in")
        n_in = sem("n_in")
        gu_hi, scaled = sem("gu_hi"), sem("scaled")
        dve_step, pool_step = sem("dve_step"), sem("pool_step")
        passed = sem("passed")
        carried = sem("carried")
        gated = sem("gated")
        cleared, shaped, counted, kset, setup, tau_step = (
            sem(n) for n in ("cleared", "shaped", "counted", "kset", "setup", "tau_step"))

        x_t = x.rearrange("b (t p) d -> b p t d", p=128)
        out_t = out.rearrange("b (t p) d -> b p t d", p=128)
        block = ctx_.enter_context(nc.Block())

        def full(u, name):
            k, n = u(name)
            return m_full[k], n + 1

        def read(u, name):
            k, n = u(name)
            return m_read[k], n + 2

        def free(u, name):
            k, n = u(name)
            return m_read[k], n + 1

        def wait_apart(engine, semaphore, value):
            engine.wait_ge(semaphore, value)
            engine.sem_inc(passed, 1)

        def score_use(it, n):
            return n % 2, it * S_USES + n // 2

        def acc_use(it, G):
            return G % 2, it * O_USES[G % 2] + G // 2

        @block.sync
        def _(sp):
            sp.dma_start(xin[:, :, :], x_t[0]).then_inc(xin_in, 16)
            sp.dma_start(pars[:, :, :], par).then_inc(par_in, 16)
            sp.dma_start(n1s[:, :], n1w).then_inc(n_in, 16)
            sp.dma_start(n2s[:, :], n2w).then_inc(n_in, 16)
            sp.dma_start(rts[:, :], router).then_inc(w_in, 16)

            def restack(names, first, bt):
                for i, name in enumerate(names):
                    sp.wait_ge(parts_ready, bt * 4 + first + i + 1)
                    sp.dma_start(scratch[name].rearrange("a p n -> p a n"), parts[(first + i) % 2][:, :, :]).then_inc(stored[name], 16)
                for name in names:
                    side = 0 if name[0] == "Q" else 1
                    sp.wait_ge(stored[name], bt * 16 + 16)
                    for c, pair in enumerate(PAIRS):
                        sp.dma_start(stack[name][HD * c:HD * c + HD, :, :],
                                     scratch[name][pair[side]].rearrange("(h d) n -> d h n", d=HD)).then_inc(stacked[name], 16)

            def maxima_rows(run):
                per, (h0, h1) = count[run], RUNS[run]
                for part in range(2):
                    row = stack["Q2"][ROW_ADD + part:ROW_ADD + part + 1, h0:h1, :]
                    sp.dma_start(row.rearrange("o h (t n) -> o (h t) n", n=128),
                                 mT[run][part * per:(part + 1) * per, :]).then_inc(row_in[run], 16)

            def prepare(u, bt, it=None):
                if it is None:
                    restack(("Q2", "K2"), 0, bt)
                    sp.wait_ge(setup, 2)
                    restack(("Q1", "K1"), 2, bt)
                else:
                    for k in range(2):
                        wait_apart(sp, s_full[k], it * S_USES + N1)
                    restack(("Q2",), 0, bt)
                    restack(("K2",), 1, bt)
                    for k in range(2):
                        wait_apart(sp, s_full[k], it * S_USES + UNITS)
                    restack(("Q1",), 2, bt)
                    restack(("K1",), 3, bt)
                wait_apart(sp, *read(u, "maxT_X"))
                maxima_rows("X")

            def row(u, it, following):
                if following:
                    wait_apart(sp, h_ready, it + 1)
                    sp.dma_start(xin[:, :, :], x_t[bass.ds(it + 1, 1)].rearrange("o p t d -> (o p) t d")).then_inc(xin_in, 16)
                sp.dma_start(xres[:, :, :], x_t[bass.ds(it, 1)].rearrange("o p t d -> (o p) t d")).then_inc(xres_in, 16)
                for run in ("Y", "Z"):
                    wait_apart(sp, *read(u, "maxT_" + run))
                    maxima_rows(run)
                if following:
                    prepare(u, it + 1, it)
                wait_apart(sp, *read(u, "outT"))
                sp.dma_start(out_t[bass.ds(it, 1)].rearrange("o p t d -> (o p) t d"), xres[:, :, :]).then_inc(written, 16)
                wait_apart(sp, written, it * 16 + 16)

            sp.wait_ge(kset, 2)
            prepare(FIRST, 0)
            with sp.Fori(0, B - 1) as it:
                row(LOOP.row(it), it, True)
            row(LAST, B - 1, False)

        @block.gpsimd
        def _(pool):
            g = nc.gpsimd
            g.memset(ident[:, :], 0.0).then_inc(cleared, 1)
            g.memset(below[:, :], 1.0).then_inc(cleared, 1)
            selv = PT[:, 2, 0:E * 128].rearrange("p (e m) -> p e m", e=E)
            g.memset(selv, 0.0).then_inc(cleared, 1)
            g.memset(bparts[:, :, :], 1.0).then_inc(cleared, 1)
            g.memset(ones[:, :], 1.0).then_inc(shaped, 1)
            g.iota(iota_i[:, :], [[1, E]], base=0, channel_multiplier=0).then_inc(counted, 1)
            g.iota(rest_i[:, :], [[-128, NT]], base=L - 1, channel_multiplier=-1).then_inc(counted, 1)
            pool.wait_ge(cleared, 4)
            g.affine_select(out=ident[:, :], in_=ident[:, :], compare_op=ALU.not_equal, fill=1.0, base=0,
                            pattern=[[-1, 128]], channel_multiplier=1).then_inc(shaped, 1)
            g.affine_select(out=below[:, :], in_=below[:, :], compare_op=ALU.is_gt, fill=0.0, base=0,
                            pattern=[[-1, 128]], channel_multiplier=1).then_inc(shaped, 1)
            g.affine_select(out=bparts[:, :, :], in_=bparts[:, :, :], compare_op=ALU.is_equal, fill=0.0, base=-ROW_ADD,
                            pattern=[[-1, 3], [0, H]], channel_multiplier=1).then_inc(shaped, 1)
            g.affine_select(out=selv, in_=selv, compare_op=ALU.not_equal, fill=1.0, base=0,
                            pattern=[[-1, E], [0, 128]], channel_multiplier=1).then_inc(cleared, 1)
            pool.wait_ge(cleared, 5)
            g.affine_select(out=selv, in_=selv, compare_op=ALU.not_equal, fill=1.0, base=-32,
                            pattern=[[-1, E], [0, 128]], channel_multiplier=1).then_inc(shaped, 1)
            g.memset(stack["K2"][:, :, :].bitcast(dt.uint32), 0x3F803F80).then_inc(kset, 1)
            g.memset(stack["Q2"][:, :, :].bitcast(dt.uint32), 0).then_inc(kset, 1)

            def split_steps(u, name, bt, following):
                i = ("Q2", "K2", "Q1", "K1").index(name)
                s, p, c = split[i % 2], parts[i % 2], bt * SPLIT_STEPS + 2 * i
                wait_apart(pool, *read(u, name))
                g.tensor_tensor(s[:, :], s[:, :], p[:, 0, :], ALU.subtract).then_inc(pool_step, 1)
                yield
                wait_apart(pool, pool_step, c + 1)
                g.tensor_tensor(p[:, 1, :], s[:, :], ones[:, 0:1].broadcast_to([128, L]), ALU.mult).then_inc(pool_step, 1)
                yield
                wait_apart(pool, pool_step, c + 2)
                g.tensor_tensor(p[:, 2, :], s[:, :], p[:, 1, :], ALU.subtract).then_inc(parts_ready, 1)
                yield

            def mask(it, n):
                wait_apart(pool, weighed, it * WEIGHED + 2 * (n - N1) + 2)
                w, blocks = width(n), len(ATTENTION[n][2])
                v = PT[:, n % SLOTS, 0:4 * w].rearrange("p (h n) -> p h n", n=w)[:, :, 0:128 * blocks]
                pattern = [[0, 4], [1, 128]] if blocks == 1 else [[0, 4], [0, 2], [1, 128]]
                g.affine_select(out=v, in_=v, compare_op=ALU.is_ge, fill=0.0, base=0,
                                pattern=pattern, channel_multiplier=-1).then_inc(masked, 1)

            def weigh_expert(it, e):
                k, c = score_use(it, 2 * (EXPERT + e) + 1)
                pool.wait_ge(s_read[k], c + 2)
                k, c = acc_use(it, 2 * NG + 2 * e - 1)
                pool.wait_ge(o_read[k], c + 2)
                a = AB[e % DEPTH].rearrange("p (f n) -> p f n", f=NFH)
                w = CB[(e - 1) % DEPTH].unsqueeze(1).broadcast_to([128, NFH, L])
                g.tensor_tensor(a, a, w, ALU.mult).then_inc(routed, 1)

            def row(u, it, following):
                wait_apart(pool, xn_ready, it + 1)
                wait_apart(pool, down_done, it * DOWNS + DEPTH)
                g.tensor_scalar(x1[:, :, :], xn[:, :, :], 1.0, None, ALU.mult).then_inc(carried, 1)
                for n in range(N1, UNITS):
                    mask(it, n)
                    if following and n == 18:
                        steps = split_steps(u, "Q2", it + 1, True)
                    if following and n == 21:
                        steps = split_steps(u, "K2", it + 1, True)
                    if following and 18 <= n < 24:
                        next(steps)
                for e in range(1, NE - 1):
                    if following and e < 3:
                        for _step in split_steps(u, ("Q1", "K1")[e - 1], it + 1, True):
                            pass
                    weigh_expert(it, e)

            pool.wait_ge(kset, 2)
            for name in ("Q2", "K2", "Q1", "K1"):
                for _step in split_steps(FIRST, name, 0, False):
                    pass
            pool.wait_ge(gu_hi, 2)
            for i in range(2):
                g.tensor_tensor(wgu_lo[:, :, i * F:i * F + F], gu_raw[i], wgu_hi[:, :, i * F:i * F + F],
                                ALU.subtract).then_inc(pv_done, SLOTS // 2)
            with pool.Fori(0, B - 1) as it:
                row(LOOP.row(it), it, True)
            row(LAST, B - 1, False)

        @block.scalar
        def _(act):
            a = nc.scalar
            act.dma_start(w2s[:, :, :], w2).then_inc(w_in, 16)
            act.dma_start(w1s[:, :, :], w1).then_inc(w_in, 16)
            def tau():
                act.wait_ge(par_in, 16)
                for raw, w in zip(gu_raw, (w_gu[:, :, 0, :], w_gu[:, :, 1, :])):
                    act.dma_start(raw, w).then_inc(gu_in, 16)
                act.dma_start(wdn[:, :, :, :], w_dn).then_inc(dn_in, 16)
                a.activation(pt[0][:, :], pars[:, 0, :], ACT.Abs).then_inc(tau_step, 1)
                act.wait_ge(tau_step, 1)
                a.activation(pt[1][:, :], pt[0][:, :], ACT.Exp, scale=-1.0).then_inc(tau_step, 1)
                act.wait_ge(tau_step, 3)
                a.activation(pt[3][:, :], pt[2][:, :], ACT.Ln).then_inc(tau_step, 1)

            def evacuate(u, name, dst, **scale):
                k, _n = u(name)
                act.wait_ge(*full(u, name))
                a.activation(dst, M[k][0:dst.shape[0], 0:dst.shape[-1]], ACT.Identity, **scale).then_inc(m_read[k], 1)

            def copy_v(u, name, V):
                k, _n = u(name)
                act.wait_ge(*full(u, name))
                a.activation(V[:, :, :, 0:HD], M[k][:, :].rearrange("p (t h d) -> p t h d", t=NT, h=H),
                             ACT.Copy).then_inc(m_read[k], 1)

            def projection(u, name, bt):
                i = ("Q2", "K2", "Q1", "K1").index(name)
                k, _n = u(name)
                scale = {"Q2": {"scale": HD ** -0.5}, "Q1": {"scale": qs1[:, :]}}.get(name, {})
                if i >= 2:
                    act.wait_ge(stored[("Q2", "K2")[i - 2]], bt * 16 + 16)
                elif not isinstance(bt, int) or bt > 0:
                    act.wait_ge(stored[("Q1", "K1")[i]], bt * 16)
                act.wait_ge(*full(u, name))
                a.activation(split[i % 2][:, :], M[k][:, :], ACT.Identity, **scale)
                a.activation(parts[i % 2][:, 0, :], M[k][:, :], ACT.Identity, **scale).then_inc(m_read[k], 1)

            def take(u, name, bt):
                if name[:5] == "maxT_":
                    evacuate(u, name, mT[name[5]][:, :])
                elif name == "xnT":
                    evacuate(u, name, xnT[:, :])
                elif name == "hT":
                    evacuate(u, name, hT[:, :], scale=n1s[:, :])
                elif name == "h2T":
                    k, _n = u(name)
                    act.wait_ge(*full(u, name))
                    a.activation(h2T[:, :], M[k][:, :], ACT.Identity, scale=n2s[:, :])
                    a.activation(h2hi[:, :], M[k][:, :], ACT.Identity, scale=n2s[:, :]).then_inc(m_read[k], 1)
                elif name in ("ctxT2", "ctxT1"):
                    evacuate(u, name, ctxT[:, :])
                elif name == "proj1":
                    evacuate(u, name, sT[:, :])
                elif name in ("V2", "V1"):
                    copy_v(u, name, V2 if name == "V2" else V1)
                elif name in ("Q2", "K2", "Q1", "K1"):
                    projection(u, name, bt)

            def acc_out(it, G):
                k, _c = acc_use(it, G)
                last = NT * G + NT - 1 if G < NG else N1 + 3 * (G - NG) + 2
                act.wait_ge(pv_done, it * UNITS + last + 1 + SLOTS)
                a.activation(OS[:, G % NG, :], O[k][:, :], ACT.Copy).then_inc(o_read[k], 1)

            def weights(it, n, q):
                w = width(n)
                if q == 0:
                    act.wait_ge(pv_done, it * UNITS + n + 1)
                if q == 0 and n in (0, 2):
                    act.wait_ge(down_done, it * DOWNS + n + 1)
                k, c = score_use(it, 2 * n + q)
                act.wait_ge(s_full[k], c + 1)
                a.activation(PT[:, n % SLOTS, 2 * q * w:2 * q * w + 2 * w].rearrange("p (r n) -> p r n", r=2),
                             S[k][:, :].rearrange("p (r n) -> p r n", r=2)[:, :, 0:w],
                             ACT.Exp if n < N1 else ACT.Sigmoid).then_inc(s_read[k], 1)

            def routing_weights(it, e):
                k, c = acc_use(it, 2 * NG + 2 * e - 1)
                act.wait_ge(cb_full, it * E + e)
                if e > DEPTH:
                    act.wait_ge(routed, it * (E - 1) + e - DEPTH)
                a.activation(CB[(e - 1) % DEPTH], O[k][:, :], ACT.Copy).then_inc(o_read[k], 1)

            def row(u, it, following):
                bt = it + 1
                outs = {**{NT * G + NT + (2 if G < NG - 1 else 1): G for G in range(NG)}, **{N1 + 3 * g + 6: NG + g for g in range(NG - 2)},
                        UNITS - 1: 2 * NG - 2}
                for n in range(UNITS):
                    names = u.places[n]
                    weights(it, n, 0)
                    for name in names[:len(names) // 2]:
                        take(u, name, bt)
                    weights(it, n, 1)
                    if n == N1 + 6:
                        act.wait_ge(*full(u, ("oT2", NT - 1)))
                    if n in outs:
                        acc_out(it, outs[n])
                    for name in names[len(names) // 2:]:
                        take(u, name, bt)
                    if n == 24:
                        act.wait_ge(*read(u, "proj2"))
                        for t in range(NT):
                            a.activation(h2t[:, t, :], x1[:, t, :], ACT.Square, accum_out=ssum[:, t:t + 1]).then_inc(squared, 1)
                act.wait_ge(*read(u, "logits"))
                a.activation(lp[:, :, :], ld[:, :, :], ACT.Sigmoid).then_inc(exps_ready, 1)
                a.activation(lq[:, :, :], ld[:, :, :], ACT.Sigmoid, scale=-1.0).then_inc(exps_ready, 1)
                for e in range(NE):
                    if e >= 2:
                        routing_weights(it, e - 1)
                    k, c = score_use(it, 2 * (EXPERT + e))
                    act.wait_ge(s_full[k], c + 1)
                    act.wait_ge(down_done, it * DOWNS + e + 1)
                    if e < DEPTH:
                        act.wait_ge(pv_done, it * UNITS + UNITS + e + 1)
                    a.activation(AB[e % DEPTH], S[k][:, :], ACT.Silu).then_inc(s_read[k], 1)
                    if e == 0:
                        acc_out(it, 2 * NG - 1)
                    for name in u.places[EXPERT + e]:
                        take(u, name, bt)
                    if e == 0:
                        act.wait_ge(gap_ready, it + 1)
                        a.activation(wgap[:, :], dtop[:, :], ACT.Tanh, scale=0.5).then_inc(top_ready, 1)
                    if e == NE - 1:
                        routing_weights(it, e)
                act.wait_ge(down_done, it * DOWNS + DOWNS + DEPTH)
                a.activation(gT[:, :], O[0][:, :], ACT.Silu).then_inc(o_read[0], 1)

            tau()
            act.wait_ge(n_in, 32)
            for n in FIRST.places:
                for name in FIRST.places[n]:
                    if name == "Q1":
                        act.wait_ge(tau_step, 5)
                        a.activation(pt[7][:, 0:H], pt[6][:, 0:H], ACT.Sigmoid).then_inc(tau_step, 1)
                        act.wait_ge(scaled, 1)
                    if name == "V2":
                        act.wait_ge(setup, 1)
                    take(FIRST, name, 0)
                    if name == "V2":
                        act.wait_ge(gu_in, 32)
                        for i in range(2):
                            a.activation(wgu_hi[:, :, i * F:i * F + F], gu_raw[i], ACT.Copy).then_inc(gu_hi, 1)
            with act.Fori(0, B - 1) as it:
                row(LOOP.row(it), it, True)
            row(LAST, B - 1, False)

        @block.vector
        def _(dve):
            v = nc.vector
            steps = [0, 0]

            def step(ins, apart=False):
                ins.then_inc(dve_step, 1)
                steps[0] += 1
                if apart:
                    wait_apart(dve, dve_step, steps[1] + steps[0])
                else:
                    dve.wait_ge(dve_step, steps[1] + steps[0])

            def norm_stats(bt):
                dve.wait_ge(xin_in, bt * 16 + 16)
                for t in range(NT):
                    last = v.bn_stats(stats[:, t, :], xin[:, t, :])
                step(last, apart=True)
                for t in range(NT):
                    last = v.bn_aggr(mv[:, t, :], stats[:, t, :])
                step(last)
                v.tensor_scalar(root[:, 0, :], mv[:, :, 1], 1e-5, None, ALU.add)
                step(v.tensor_scalar(root[:, 1, :], mv[:, :, 1], 1.0 + 1e-6, 1e-11, ALU.mult, ALU.add))
                inverse_root(rinv[:, 0:2, :], root[:, 0:2, :], newton[:, :, :])

            def inverse_root(y, x, t):
                step(v.tensor_scalar(y.bitcast(dt.int32), x.bitcast(dt.int32), 1, None, ALU.logical_shift_right))
                step(v.tensor_scalar(y.bitcast(dt.int32), y.bitcast(dt.int32), -1.0, 1597463007.0, ALU.mult, ALU.add))
                for _i in range(3):
                    step(v.tensor_tensor(t, y, x, ALU.mult))
                    step(v.scalar_tensor_tensor(t, t, -0.5, y, ALU.mult, ALU.mult))
                    step(v.scalar_tensor_tensor(y, t, 1.5, y, ALU.add, ALU.mult))

            def norm_apply(bt):
                for dst, i, ready in ((xn, 0, xn_ready), (ht, 1, h_ready)):
                    for t in range(NT):
                        last = v.tensor_scalar(dst[:, t, :], xin[:, t, :], mv[:, t, 0:1], rinv[:, i, t:t + 1],
                                               ALU.subtract, ALU.mult)
                    last.then_inc(ready, 1)

            def maximum(u, name):
                _m, h, t = name
                k, _n = u(name)
                dve.wait_ge(*full(u, name))
                v.tensor_reduce(nmax[:, h, t:t + 1], M[k][:, :], AX.X, ALU.max, negate=True).then_inc(m_read[k], 1)

            def maxima_parts(u, run):
                blocks, dst, ready = MAX[run], mh[run], max_ready[run]
                for b in blocks[-2:]:
                    dve.wait_ge(*read(u, b))
                h0, h1 = blocks[0][1], blocks[-1][1] + 1
                src = nmax[:, h0:h1, :].rearrange("p h t -> p (h t)")
                step(v.tensor_copy(dst[:, 0, :], src))
                v.tensor_tensor(dst[:, 1, :], src, dst[:, 0, :], ALU.subtract).then_inc(ready, 1)

            def attention_out(u, name, t):
                k, _n = u((name, t))
                w = M[k][:, :].rearrange("p (g q c) -> p (g q) c", g=NG, c=32)
                dve.wait_ge(*full(u, (name, t)))
                if name == "oT1":
                    step(v.tensor_tensor(dsum[:, t, :], w[:, :, HD], dcorr[:, t, :], ALU.add))
                    v.tensor_tensor(corr[:, t, :].rearrange("p (h d) -> p h d", h=H), w[:, :, 0:HD],
                                    corr[:, t, :].rearrange("p (h d) -> p h d", h=H), ALU.add).then_inc(m_read[k], 1)
                    step(v.reciprocal(rden[:, t, :], dsum[:, t, :]))
                    dve.wait_ge(*read(u, (name, t)))
                    v.tensor_tensor(ctxs[:, t, :].rearrange("p (h d) -> p h d", h=H),
                                    corr[:, t, :].rearrange("p (h d) -> p h d", h=H),
                                    rden[:, t, :].unsqueeze(2).broadcast_to([128, H, HD]), ALU.mult).then_inc(gated, 1)
                else:
                    step(v.reciprocal(rden[:, t, :], w[:, :, HD]))
                    v.tensor_tensor(ctxs[:, t, :].rearrange("p (h d) -> p h d", h=H), w[:, :, 0:HD],
                                    rden[:, t, :].unsqueeze(2).broadcast_to([128, H, HD]), ALU.mult).then_inc(m_read[k], 1)

            def weigh(it, n, q):
                k, c = score_use(it, 2 * n + q)
                dve.wait_ge(s_read[k], c + 2)
                w = width(n)
                p = PT[:, n % SLOTS, 2 * q * w:2 * q * w + 2 * w]
                v.scalar_tensor_tensor(p, p, 1.0, p, ALU.subtract, ALU.mult).then_inc(weighed, 1)

            def router(u, it):
                dve.wait_ge(exps_ready, 2 * it + 2)
                step(v.reciprocal(lq[:, :, :], lq[:, :, :]))
                step(v.tensor_tensor(lp[:, :, :], lp[:, :, :], lq[:, :, :], ALU.mult))
                step(v.tensor_reduce(lsum[:, :], lp[:, :, :], AX.X, ALU.add))
                step(v.reciprocal(lsum[:, :], lsum[:, :]))
                step(v.tensor_tensor(lp[:, :, :], lp[:, :, :], lsum[:, :].unsqueeze(2).broadcast_to([128, NT, E]), ALU.mult), apart=True)
                for t in range(NT):
                    last = v.max(top[:, t, :], lp[:, t, :])
                step(last)
                v.tensor_tensor(dtop[:, :], top[:, :, 0], top[:, :, 1], ALU.subtract).then_inc(gap_ready, 1)
                for t in range(NT):
                    last = v.max_index(topi[:, t, :], top[:, t, :], lp[:, t, :])
                step(last)
                step(v.tensor_copy(topf[:, :, :], topi[:, :, :]))

            def combine(it):
                dve.wait_ge(top_ready, it + 1)
                for i, half in ((0, 0.5), (1, -0.5)):
                    last = v.tensor_scalar(wtop[:, i, :], wgap[:, :], half, 0.5, ALU.mult, ALU.add)
                step(last)
                shape = [128, NT, E]
                for i, dst in ((0, lp), (1, lq)):
                    step(v.tensor_tensor(dst[:, :, :], iota_f[:, :].unsqueeze(1).broadcast_to(shape),
                                         topf[:, :, i:i + 1].broadcast_to(shape), ALU.is_equal))
                    step(v.tensor_tensor(dst[:, :, :], dst[:, :, :], wtop[:, i, :].unsqueeze(2).broadcast_to(shape), ALU.mult))
                v.tensor_tensor(comb[:, :, :], lp[:, :, :], lq[:, :, :], ALU.add).then_inc(comb_ready, 1)

            def take(u, it, name):
                k, _n = u(name)
                if name[0] == "max":
                    maximum(u, name)
                elif name[0] in ("oT1", "oT2"):
                    if name == ("oT1", 0):
                        dve.wait_ge(*read(u, "suffix"))
                    attention_out(u, *name)
                elif name == "proj2":
                    dve.wait_ge(*full(u, name))
                    dve.wait_ge(carried, it + 1)
                    v.tensor_tensor(x1[:, :, :].rearrange("p t d -> p (t d)"), M[k][:, :],
                                    x1[:, :, :].rearrange("p t d -> p (t d)"), ALU.add).then_inc(m_read[k], 1)
                elif name == "logits":
                    dve.wait_ge(*full(u, name))
                    lg = M[k][:, 0:NT * E].rearrange("p (t e) -> p t e", t=NT)
                    step(v.tensor_reduce(lmax[:, :], lg, AX.X, ALU.max))
                    v.tensor_tensor(ld[:, :, :], lg, lmax[:, :].unsqueeze(2).broadcast_to([128, NT, E]),
                                    ALU.subtract).then_inc(m_read[k], 1)
                    router(u, it)
                elif name == "suffix":
                    dve.wait_ge(*full(u, name))
                    v.tensor_tensor(corr[:, :, :].rearrange("p t (h d) -> p t h d", h=H),
                                    M[k][:, :].rearrange("p (t h d) -> p t h d", t=NT, h=H),
                                    cneg[:, :].unsqueeze(1).unsqueeze(3).broadcast_to([128, NT, H, HD]),
                                    ALU.mult).then_inc(m_read[k], 1)
                elif name == "combT":
                    dve.wait_ge(*full(u, name))
                    step(v.tensor_copy(cT[0:E, :], M[k][0:E, :]))
                    v.tensor_tensor(cT[32:32 + E, :], M[k][0:E, :], cT[0:E, :], ALU.subtract).then_inc(m_read[k], 1)

            last_x = max(n for n, names in PLACES.items() if MAX["X"][-1] in names)

            def row(u, it, following):
                bt = it + 1
                steps[0] = 0
                for n in range(N1):
                    for name in u.places[n]:
                        take(u, it, name)
                    if n == 4:
                        maxima_parts(u, "Y")
                    if n == 8:
                        maxima_parts(u, "Z")
                if following:
                    norm_stats(bt)
                    dve.wait_ge(carried, it + 1)
                    norm_apply(bt)
                for n in range(N1, UNITS):
                    weigh(it, n, 0)
                    for name in u.places[n]:
                        if name != "logits":
                            take(u, it, name)
                    if n == 24:
                        dve.wait_ge(squared, (it + 1) * NT)
                        step(v.tensor_scalar(root[:, 2, :], ssum[:, :], 1.0 / D, 1e-6, ALU.mult, ALU.add))
                        inverse_root(rinv[:, 2, :], root[:, 2, :], newton[:, 0, :])
                        for t in range(NT):
                            last = v.tensor_scalar(h2t[:, t, :], x1[:, t, :], rinv[:, 2, t:t + 1], None, ALU.mult)
                        last.then_inc(h2_ready, 1)
                    if n == 26:
                        dve.wait_ge(*read(u, "h2T"))
                        v.tensor_tensor(h2lo[:, :], h2T[:, :], h2hi[:, :], ALU.subtract).then_inc(h2r_ready, 1)
                    weigh(it, n, 1)
                take(u, it, "logits")
                for e in range(NE):
                    work = u.places[EXPERT + e]
                    early = len(work) * 4 // 6 if e > 1 else 2
                    if e > 0:
                        for name in work[:early]:
                            take(u, it, name)
                    k, c = score_use(it, 2 * (EXPERT + e))
                    k2, c2 = score_use(it, 2 * (EXPERT + e) + 1)
                    dve.wait_ge(s_read[k], c + 2)
                    dve.wait_ge(s_full[k2], c2 + 1)
                    v.tensor_tensor(AB[e % DEPTH], AB[e % DEPTH], S[k2][:, :], ALU.mult).then_inc(s_read[k2], 1)
                    if e == 0:
                        take(u, it, "suffix")
                        combine(it)
                    if e > 0:
                        for name in work[early:]:
                            take(u, it, name)
                    if following and EXPERT + e == last_x:
                        maxima_parts(u, "X")
                dve.wait_ge(s_read[1], it * S_USES + S_USES + 1)
                k, c = acc_use(it, 2 * NG + 2 * (NE - 1) - 1)
                dve.wait_ge(o_read[k], c + 2)
                v.tensor_tensor(AB[(NE - 1) % DEPTH].rearrange("p (f n) -> p f n", f=NFH),
                                AB[(NE - 1) % DEPTH].rearrange("p (f n) -> p f n", f=NFH),
                                CB[(NE - 2) % DEPTH].unsqueeze(1).broadcast_to([128, NFH, L]), ALU.mult).then_inc(routed_last, 1)
                dve.wait_ge(o_read[0], it * O_USES[0] + O_USES[0] + 1)
                dve.wait_ge(*read(u, "proj1"))
                v.tensor_tensor(gT[:, :], gT[:, :], sT[:, :], ALU.mult).then_inc(prod_ready, 1)
                k, _n = u("outT")
                dve.wait_ge(*full(u, "outT"))
                dve.wait_ge(xres_in, it * 16 + 16)
                v.tensor_tensor(xres[:, :, :].rearrange("p t d -> p (t d)"), M[k][:, :],
                                xres[:, :, :].rearrange("p t d -> p (t d)"), ALU.add).then_inc(m_read[k], 1)
                assert steps[0] <= DVE_ROW and (not following or steps[0] == DVE_ROW), steps

            for k in range(2):
                dve.sem_inc(m_read[k], 1)
                dve.sem_inc(s_read[k], 1)
            norm_stats(0)
            norm_apply(0)
            dve.wait_ge(tau_step, 2)
            v.tensor_scalar(pt[2][:, :], pt[1][:, :], 1.0, None, ALU.add).then_inc(tau_step, 1)
            v.memset(V2[:, :, :, :], 0.0)
            v.memset(V1[:, :, :, :], 0.0)
            step(v.memset(cT[:, :].bitcast(fp32), 0.0))
            v.memset(V2[:, :, :, HD:HD + 1], 1.0)
            v.memset(V1[:, :, :, HD:HD + 1], 1.0).then_inc(setup, 1)
            dve.wait_ge(tau_step, 4)
            step(v.tensor_scalar(pt[4][:, :], pt[2][:, :], -1.0, None, ALU.add))
            step(v.tensor_scalar(pt[5][:, :], pt[4][:, :], 0.0, None, ALU.is_equal))
            step(v.tensor_tensor(pt[6][:, :], pt[4][:, :], pt[5][:, :], ALU.add))
            step(v.reciprocal(pt[6][:, :], pt[6][:, :]))
            step(v.tensor_tensor(pt[6][:, :], pt[6][:, :], pt[3][:, :], ALU.mult))
            step(v.tensor_tensor(pt[6][:, :], pt[6][:, :], pt[5][:, :], ALU.add))
            step(v.tensor_tensor(pt[6][:, :], pt[6][:, :], pt[1][:, :], ALU.mult))
            step(v.scalar_tensor_tensor(pt[6][:, :], pars[:, 0, :], 0.0, pt[6][:, :], ALU.max, ALU.add))
            step(v.tensor_scalar(pt[6][:, :], pt[6][:, :], 1e-6, None, ALU.add))
            step(v.reciprocal(pt[5][:, :], pt[6][:, :]))
            step(v.tensor_scalar(pt[3][:, :], pt[5][:, :], 2.0, None, ALU.mult))
            v.tensor_scalar(qs1[:, :], pt[3][:, H:H + 1], HD ** -0.5, None, ALU.mult).then_inc(scaled, 1)
            step(v.scalar_tensor_tensor(pt[4][:, :], pars[:, 1, :], -1.0, pt[3][:, :], ALU.mult, ALU.mult))
            v.scalar_tensor_tensor(pt[6][:, :], pt[3][:, :], MASKED, pt[4][:, :], ALU.mult, ALU.add).then_inc(tau_step, 1)
            step(v.tensor_copy(bsplit[:, 0, :], pt[4][:, 0:H]))
            step(v.tensor_tensor(pt[5][:, 0:H], pt[4][:, 0:H], bsplit[:, 0, :], ALU.subtract))
            step(v.tensor_copy(bsplit[:, 1, :], pt[5][:, 0:H]))
            step(v.tensor_tensor(bsplit[:, 2, :], pt[5][:, 0:H], bsplit[:, 1, :], ALU.subtract))
            for k in range(2):
                v.memset(O[k][:, :], 0.0).then_inc(o_read[k], 1)
            v.memset(stack["K1"][:, :, :].bitcast(dt.uint32), 0x3F803F80)
            v.memset(stack["Q1"][:, :, :].bitcast(dt.uint32), 0).then_inc(setup, 1)
            dve.wait_ge(shaped, 5)
            step(v.tensor_tensor(bparts[:, :, :], bparts[:, :, :], bsplit[:, :, :], ALU.mult))
            dve.wait_ge(counted, 2)
            v.tensor_copy(iota_f[:, :], iota_i[:, :])
            step(v.tensor_copy(rest_f[:, :], rest_i[:, :]))
            dve.wait_ge(tau_step, 6)
            step(v.scalar_tensor_tensor(cneg[:, :], pt[7][:, 0:H], 1.0, pt[7][:, 0:H], ALU.subtract, ALU.mult))
            step(v.tensor_tensor(dcorr[:, :, :], rest_f[:, :].unsqueeze(2).broadcast_to([128, NT, H]),
                                 cneg[:, :].unsqueeze(1).broadcast_to([128, NT, H]), ALU.mult))
            step(v.tensor_scalar(dcorr[:, :, :], dcorr[:, :, :], -2.5e-7, None, ALU.add))
            step(v.tensor_copy(identb[:, :], ident[:, :]))
            v.tensor_copy(sel[:, :, :], PT[:, 2, 0:E * 128].rearrange("p (e m) -> p e m", e=E))
            dve.sem_inc(down_done, DEPTH)
            for name in MAX["X"]:
                maximum(FIRST, name)
            maxima_parts(FIRST, "X")
            step(v.tensor_reduce(brow[:, :], bparts[:, :, :].rearrange("p a h -> p h a"), AX.X, ALU.add))
            dve.wait_ge(setup, 2)
            v.tensor_copy(stack["Q1"][ROW_ADD:ROW_ADD + 32, :, :],
                          brow[ROW_ADD:ROW_ADD + 32, :].unsqueeze(2).broadcast_to([32, H, L])).then_inc(setup, 1)
            assert steps[0] == DVE_FIRST, steps[0]
            steps[1] = DVE_FIRST
            with dve.Fori(0, B - 1) as it:
                steps[1] = DVE_FIRST + it * DVE_ROW
                row(LOOP.row(it), it, True)
            steps[1] = DVE_FIRST + (B - 1) * DVE_ROW
            row(LAST, B - 1, False)

        @block.tensor
        def _(pe):
            t_ = nc.tensor
            order, current = [], [None]

            def begin(u, name):
                order.append(name)
                assert u.order[len(order) - 1] == name, (name, u.order[len(order) - 1])
                k, _n = u(name)
                pe.wait_ge(*free(u, name))
                return k

            def transposed(u, name, src):
                k = begin(u, name)
                for t in range(NT):
                    last = t_.transpose(M[k][:, t * 128:t * 128 + 128], src[:, t, :], ident[:, :])
                last.then_inc(m_full[k], 1)

            def projected(u, name, w, src):
                k = begin(u, name)
                t_.matmul(M[k][:, :], w, src[:, :], start=True, stop=True).then_inc(m_full[k], 1)

            def projected_v(u, name, w, src):
                k = begin(u, name)
                for t in range(NT):
                    last = t_.matmul(M[k][:, t * 128:t * 128 + 128], src[:, t * 128:t * 128 + 128], w, start=True, stop=True)
                last.then_inc(m_full[k], 1)

            def maximum(u, name):
                k = begin(u, name)
                _m, h, t = name
                t_.matmul(M[k][:, :], stack["Q2"][0:ROW_ADD, h, t * 128:t * 128 + 128], stack["K2"][0:ROW_ADD, h, :],
                          start=True, stop=True).then_inc(m_full[k], 1)

            def maxima_T(u, name, src, ready, n):
                pe.wait_ge(ready, n + 1)
                k = begin(u, name)
                t_.matmul(M[k][0:src.shape[1] * src.shape[2], 0:128], src[:, :, :], identb[:, :], start=True, stop=True)\
                    .then_inc(m_full[k], 1)

            def out_T(u, name, t):
                k = begin(u, (name, t))
                for hg in range(NG):
                    last = t_.transpose(M[k][:, hg * 128:hg * 128 + 128], OS[:, hg, t * 128:t * 128 + 128], ident[:, :])
                last.then_inc(m_full[k], 1)

            def scores(it, n, q):
                k, c = score_use(it, 2 * n + q)
                pe.wait_ge(s_read[k], c + 1)
                g, _kind, js = ATTENTION[n]
                key, query = ("K2", "Q2") if n < N1 else ("K1", "Q1")
                for r in range(2):
                    h, at = 4 * g + 2 * q + r, 512 * r
                    for j in js:
                        i0 = 0 if n < N1 else 128 * j
                        last = t_.matmul(S[k][:, at:at + L - i0], stack[key][:, h, 128 * j:128 * j + 128],
                                         stack[query][:, h, i0:L], start=True, stop=True)
                        at += L - i0
                last.then_inc(s_full[k], 1)

            def with_v(it, n, half=None):
                g, _kind, js = ATTENTION[n]
                G, V, w = (g, V2, width(n)) if n < N1 else (NG + g, V1, width(n))
                k, c = acc_use(it, G)
                if js[0] == 0:
                    pe.wait_ge(o_read[k], c + 1)
                if n >= N1:
                    pe.wait_ge(masked, it * len(STAGE2) + n - N1 + 1)
                elif half != 1:
                    for i in range(2):
                        pe.wait_ge(s_read[i], it * S_USES + n + 2)
                at = 0
                for j in js:
                    i0, i1 = (128 * j if n >= N1 else 0, L) if half is None else (half * L // 2, (half + 1) * L // 2)
                    if n < N1:
                        at = i0
                    for q in range(4):
                        last = t_.matmul(O[k][32 * q:32 * q + VW, i0:i1], V[:, j, 4 * g + q, :],
                                         PT[:, n % SLOTS, w * q + at:w * q + at + i1 - i0],
                                         start=(j == 0), stop=(NT - 1 in js and j == js[-1] and half != 0))
                    at += i1 - i0
                if half != 0:
                    last.then_inc(pv_done, 1)

            def routing_weights(it, e):
                k, c = acc_use(it, 2 * NG + 2 * e - 1)
                pe.wait_ge(o_read[k], c + 1)
                t_.matmul(O[k][:, :], sel[:, e - 1, :], cT[:, :], start=True, stop=True).then_inc(cb_full, 1)

            def second_product(it, e):
                if e == 0:
                    pe.wait_ge(o_read[0], it * O_USES[0] + NG + 1)
                    k, c = score_use(it, 2 * EXPERT + 1)
                    pe.wait_ge(s_read[k], c + 2)
                else:
                    pe.wait_ge(*((routed, it * (E - 1) + e) if e < NE - 1 else (routed_last, it + 1)))
                for f in range(NFH):
                    last = t_.matmul(O[0][:, :], wdn[:, e, f, :], AB[e % DEPTH][:, f * 512:f * 512 + 512],
                                     start=(e == 0 and f == 0), stop=(e == NE - 1 and f == NFH - 1))
                    if f == 0:
                        yield
                last.then_inc(down_done, 1)
                yield

            def expert(it, e):
                for i in range(2):
                    k, c = score_use(it, 2 * (EXPERT + e) + i)
                    pe.wait_ge(s_read[k], c + 1)
                    for f in range(NFH):
                        cols = slice(i * F + f * 128, i * F + f * 128 + 128)
                        dst = S[k][:, f * 512:f * 512 + 512]
                        t_.matmul(dst, wgu_hi[:, e, cols], h2hi[:, :], start=True, stop=False)
                        t_.matmul(dst, wgu_hi[:, e, cols], h2lo[:, :], start=False, stop=False)
                        last = t_.matmul(dst, wgu_lo[:, e, cols], h2hi[:, :], start=False, stop=True)
                        if f == NFH - 1:
                            last.then_inc(s_full[k], 1)
                        if i == 0 and f == 0 and e >= 2:
                            if e == 2:
                                pe.wait_ge(*read(current[0], "combT"))
                            routing_weights(it, e - 1)
                        yield
                if e >= 2:
                    yield from second_product(it, e - 2)

            def wait_read(u, earlier, name):
                if u(earlier)[0] != u(name)[0]:
                    pe.wait_ge(*read(u, earlier))

            def work(u, it, name):
                bt = it + 1
                if name[0] == "max":
                    if name == MAX["X"][0]:
                        for n in ("Q2", "K2"):
                            pe.wait_ge(stacked[n], (bt + 1) * 16 * len(PAIRS))
                    maximum(u, name)
                elif name[:5] == "maxT_":
                    run = name[5]
                    maxima_T(u, name, mh[run], max_ready[run], bt if run == "X" else it)
                elif name == "xnT":
                    pe.wait_ge(xn_ready, bt + 1)
                    transposed(u, name, xn)
                elif name == "hT":
                    pe.wait_ge(h_ready, bt + 1)
                    transposed(u, name, ht)
                elif name in ("Q2", "K2", "Q1", "K1"):
                    if name == "Q2":
                        if u is FIRST:
                            pe.wait_ge(w_in, 48)
                        wait_read(u, "xnT", name)
                        wait_read(u, "hT", name)
                    w, src = (w2s, hT) if name[1] == "2" else (w1s, xnT)
                    projected(u, name, w[:, 0 if name[0] == "Q" else 1, :], src)
                elif name in ("V2", "V1"):
                    projected_v(u, name, (w2s if name == "V2" else w1s)[:, 2, :], hT if name == "V2" else xnT)
                elif name[0] in ("oT2", "oT1"):
                    if name[1] == 0:
                        done = NG // 2 if name[0] == "oT2" else NG
                        pe.wait_ge(o_read[0], it * O_USES[0] + done + 1)
                        pe.wait_ge(o_read[1], it * O_USES[1] + done + 1)
                    out_T(u, *name)
                elif name == "ctxT2":
                    wait_read(u, ("oT2", NT - 2), name)
                    wait_read(u, ("oT2", NT - 1), name)
                    transposed(u, name, ctxs)
                elif name == "ctxT1":
                    pe.wait_ge(gated, (it + 1) * NT)
                    transposed(u, name, ctxs)
                elif name in ("proj2", "proj1"):
                    wait_read(u, "ctxT" + name[4], name)
                    if name == "proj2":
                        projected_v(u, name, w2s[:, 3, :], ctxT)
                    else:
                        projected(u, name, w1s[:, 3, :], ctxT)
                elif name == "h2T":
                    pe.wait_ge(h2_ready, it + 1)
                    transposed(u, name, h2t)
                elif name == "logits":
                    wait_read(u, "h2T", name)
                    k = begin(u, name)
                    for t in range(NT):
                        last = t_.matmul(M[k][:, t * E:t * E + E], h2T[:, t * 128:t * 128 + 128], rts[:, :], start=True, stop=True)
                    last.then_inc(m_full[k], 1)
                elif name == "suffix":
                    k = begin(u, name)
                    for t in range(NT):
                        for j in range(t, NT):
                            last = t_.matmul(M[k][:, t * 128:t * 128 + 128], (below if j == t else ones)[:, :],
                                             V1[:, j, :, 0:HD], start=(j == t), stop=(j == NT - 1))
                    last.then_inc(m_full[k], 1)
                elif name == "combT":
                    pe.wait_ge(comb_ready, it + 1)
                    k = begin(u, name)
                    for t in range(NT):
                        last = t_.matmul(M[k][0:E, t * 128:t * 128 + 128], comb[:, t, :], ident[:, :], start=True, stop=True)
                    last.then_inc(m_full[k], 1)
                elif name == "outT":
                    pe.wait_ge(prod_ready, it + 1)
                    k = begin(u, name)
                    for t in range(NT):
                        last = t_.transpose(M[k][:, t * 128:t * 128 + 128], gT[:, t * 128:t * 128 + 128], ident[:, :])
                    last.then_inc(m_full[k], 1)

            def first_scores(it):
                pe.wait_ge(row_in["X"], (it + 1) * 32)
                for q in range(2):
                    scores(it, 0, q)

            def row(u, it, following):
                order.clear()
                current[0] = u
                v_at = {n: n - 2 for n in range(2, N1 + 2)} | {n: n - 3 for n in range(N1 + 3, UNITS)}
                for n in range(UNITS):
                    if n == N1 - 1:
                        pe.wait_ge(setup, 3)
                    for run, (h0, _h1) in RUNS.items():
                        if n == NT * (h0 // 4) and n:
                            pe.wait_ge(row_in[run], (it + 1) * 32)
                    if n == N1:
                        for name in ("Q1", "K1"):
                            pe.wait_ge(stacked[name], (it + 1) * 16 * len(PAIRS))
                    names = u.places[n]
                    for i in range(4):
                        if i % 2 == 0:
                            if n:
                                scores(it, n, i // 2)
                        elif v_at.get(n, N1) < N1 and v_at[n] % NT > 0:
                            with_v(it, v_at[n], i // 2)
                        elif n in v_at and i == 1:
                            with_v(it, v_at[n])
                        for name in names[len(names) * i // 4:len(names) * (i + 1) // 4]:
                            work(u, it, name)
                with_v(it, UNITS - 3)
                pe.wait_ge(h2r_ready, it + 1)
                for e in range(NE):
                    names = u.places[EXPERT + e]
                    steps = 6 if e >= 2 else 4
                    for i, _step in enumerate(expert(it, e)):
                        if e == 0 and i < 2:
                            with_v(it, UNITS - 2 + i)
                        for name in names[len(names) * i // steps:len(names) * (i + 1) // steps]:
                            work(u, it, name)
                routing_weights(it, NE - 1)
                for _step in second_product(it, NE - 2):
                    pass
                for t in range(NT):
                    last = t_.matmul(O[0][:, t * 128:t * 128 + 128], x1[:, t, :], ident[:, :], start=False, stop=False)
                last.then_inc(down_done, 1)
                for _step in second_product(it, NE - 1):
                    pass
                if following:
                    first_scores(it + 1)
                work(u, it, "outT")
                assert order == u.order

            pe.wait_ge(shaped, 5)
            for n in FIRST.places:
                for name in FIRST.places[n]:
                    work(FIRST, -1, name)
            pe.wait_ge(dn_in, 16)
            pe.wait_ge(pv_done, SLOTS)
            first_scores(0)
            with pe.Fori(0, B - 1) as it:
                row(LOOP.row(it), it, True)
            row(LAST, B - 1, False)


_INS = ["x", "par", "n1w", "n2w", "w1", "w2", "router", "w_gu", "w_dn"]


def kernel(L0_attn_x, L0_attn_Wq, L0_attn_Wk, L0_attn_Wv, L0_attn_Wo, L0_attn_compressibility, L0_attn_phase_threshold,
           L0_ffn_norm1_w, L0_ffn_norm2_w, L0_ffn_wq, L0_ffn_wk, L0_ffn_wv, L0_ffn_wo, L0_ffn_router_w,
           L0_ffn_sh_gate, L0_ffn_sh_up, L0_ffn_sh_down, L0_ffn_e_gate, L0_ffn_e_up, L0_ffn_e_down):
    import numpy as np
    import concourse.bacc as bacc
    from concourse import mybir as mb
    from concourse.bass_utils import run_bass_kernel_spmd

    def per_head(v):
        v = np.asarray(v).reshape(H)
        return np.concatenate([np.broadcast_to(v, (128, H)), np.repeat(v, HD)[:, None]], axis=1)

    gate = np.concatenate([np.asarray(L0_ffn_sh_gate)[None], np.asarray(L0_ffn_e_gate)])
    up = np.concatenate([np.asarray(L0_ffn_sh_up)[None], np.asarray(L0_ffn_e_up)])
    down = np.concatenate([np.asarray(L0_ffn_sh_down)[None], np.asarray(L0_ffn_e_down)])
    arrays = {
        "x": np.asarray(L0_attn_x),
        "par": np.stack([per_head(L0_attn_compressibility), per_head(L0_attn_phase_threshold)], axis=1),
        "n1w": np.asarray(L0_ffn_norm1_w)[:, None],
        "n2w": np.asarray(L0_ffn_norm2_w)[:, None],
        "w1": np.stack([np.asarray(w).T for w in (L0_attn_Wq, L0_attn_Wk, L0_attn_Wv, L0_attn_Wo)], axis=1),
        "w2": np.stack([np.asarray(w) for w in (L0_ffn_wq, L0_ffn_wk, L0_ffn_wv, L0_ffn_wo)], axis=1),
        "router": np.asarray(L0_ffn_router_w),
        "w_gu": np.stack([gate, up], axis=1).transpose(2, 0, 1, 3),
        "w_dn": down.reshape(NE, NFH, 128, D).transpose(2, 0, 1, 3),
    }
    arrays = {n: np.ascontiguousarray(a) for n, a in arrays.items()}
    nc = bacc.Bacc("TRN2", target_bir_lowering=False, num_devices=1)
    args = [nc.dram_tensor("in_" + n, arrays[n].shape, mb.dt.from_np(arrays[n].dtype), kind="ExternalInput").ap() for n in _INS]
    out = nc.dram_tensor("out_0", (B, L, D), mb.dt.float32, kind="ExternalOutput").ap()
    program(nc, *args, out)
    r = run_bass_kernel_spmd(nc, [{"in_" + n: arrays[n] for n in _INS}], core_ids=[0])
    return r.results[0]["out_0"]
```
